# Optimizing a Trainium2 kernel written in Bass

```python
import numpy as np
import jax
import jax.numpy as jnp

def _softmax(x, axis=-1):
    return jax.nn.softmax(x, axis=axis)

def _gelu(x):
    return jax.nn.gelu(x, approximate=True)

def _silu(x):
    return jax.nn.silu(x)

def _sigmoid(x):
    return jax.nn.sigmoid(x)

def _layernorm(x, axis=-1, eps=1e-05):
    m = jnp.mean(x, axis=axis, keepdims=True)
    v = jnp.var(x, axis=axis, keepdims=True)
    return (x - m) / jnp.sqrt(v + eps)

def _scatter_add(tgt, idx, src, axis=0):
    return tgt.at[idx].add(src)

def _segment_sum(src, seg, n):
    return jax.ops.segment_sum(src, seg, n)
kernel_name = 'mk_lm_tower_d1_tok_ids768_r4_59d24d'

def setup_inputs(seed: int=0):
    np.random.seed(seed)
    _w = jnp.asarray

    def _rec_inputs():
        import jax
        import jax.numpy as jnp
        _rk = jax.random.key(seed)
        x = jax.random.randint(jax.random.fold_in(_rk, 1), (8, 256), 0, 70, jnp.int32)
        return x
    x = _rec_inputs()

    def _L0_tok_setup():
        import jax, jax.numpy as jnp
        import numpy as np
        import math
        D_MODEL = 192
        BASE = D_MODEL // 3

        def positional_encoding(seq_length, d_model, dtype=jnp.float32):
            pos = jnp.arange(seq_length, dtype=dtype)[:, None]
            i_even = jnp.arange(0, d_model, 2, dtype=dtype)
            inv = jnp.exp(-(i_even / d_model) * math.log(10000.0))
            ang = pos * inv
            pe = jnp.stack([jnp.sin(ang), jnp.cos(ang)], axis=-1)
            return pe.reshape(seq_length, d_model)
        key = jax.random.key(seed)
        k_tok, k_c, k_s, k_q, k_sp = jax.random.split(key, 5)
        tokens = jax.random.randint(k_tok, (64, 512), 0, 70, dtype=jnp.int64)
        scale = 1.0
        color_W = jax.random.normal(k_c, (4, BASE), dtype=jnp.float32) * scale
        shape_W = jax.random.normal(k_s, (4, BASE), dtype=jnp.float32) * scale
        quantity_W = jax.random.normal(k_q, (4, BASE), dtype=jnp.float32) * scale
        special_W = jax.random.normal(k_sp, (6, D_MODEL), dtype=jnp.float32) * scale
        return {'tokens': tokens, 'color_W': color_W, 'shape_W': shape_W, 'quantity_W': quantity_W, 'special_W': special_W}
    _L0_tok_all = _L0_tok_setup()
    _L0_tok_in = {k: v for k, v in _L0_tok_all.items() if k in ('color_W', 'shape_W', 'quantity_W', 'special_W')}
    del _L0_tok_all

    def _L0_attn_setup():
        import jax, jax.numpy as jnp
        import numpy as np
        B, N, DIM = (16, 577, 192)
        HEADS, HEAD_DIM = (12, 64)
        QKV_DIM = HEADS * HEAD_DIM
        MAX_REL = 14
        TABLE_ROWS = 2 * MAX_REL + 2

        def _rel_indices(n, max_rel):
            m = n - 1
            side = int(m ** 0.5)
            r = np.arange(m)
            dv = r[None, :] // side - r[:, None] // side
            dh = r[None, :] % side - r[:, None] % side
            iv = np.clip(dv, -max_rel, max_rel) + max_rel + 1
            ih = np.clip(dh, -max_rel, max_rel) + max_rel + 1
            iv = np.pad(iv, ((1, 0), (1, 0)))
            ih = np.pad(ih, ((1, 0), (1, 0)))
            return (jnp.asarray(iv), jnp.asarray(ih))
        key = jax.random.key(seed)
        ks = jax.random.split(key, 8)
        return {'x': jax.random.normal(ks[0], (B, N, DIM), jnp.float32), 'qkv_w': jax.random.normal(ks[1], (3 * QKV_DIM, DIM), jnp.float32) * 0.02, 'proj_w': jax.random.normal(ks[2], (DIM, QKV_DIM), jnp.float32) * 0.02, 'proj_b': jnp.zeros((DIM,), jnp.float32), 'tab_kv': jax.random.normal(ks[3], (TABLE_ROWS, HEAD_DIM), jnp.float32) * 0.02, 'tab_kh': jax.random.normal(ks[4], (TABLE_ROWS, HEAD_DIM), jnp.float32) * 0.02, 'tab_vv': jax.random.normal(ks[5], (TABLE_ROWS, HEAD_DIM), jnp.float32) * 0.02, 'tab_vh': jax.random.normal(ks[6], (TABLE_ROWS, HEAD_DIM), jnp.float32) * 0.02}
    _L0_attn_all = _L0_attn_setup()
    _L0_attn_in = {k: v for k, v in _L0_attn_all.items() if k in ('qkv_w', 'proj_w', 'proj_b', 'tab_kv', 'tab_kh', 'tab_vv', 'tab_vh')}
    del _L0_attn_all

    def _L0_ffn_setup():
        import jax, jax.numpy as jnp
        import numpy as np
        B, S, D_IN, D_HID, D_OUT = (32, 128, 192, 768, 192)
        key = jax.random.key(seed)
        k1, k2, k3, k4 = jax.random.split(key, 4)
        init_k = float(np.sqrt(1.0 / D_IN))
        init_k2 = float(np.sqrt(1.0 / D_HID))
        x = jax.random.normal(k1, (B, S, D_IN), dtype=jnp.float32)
        in_weight = jax.random.uniform(k2, (D_HID, D_IN), dtype=jnp.float32, minval=-init_k, maxval=init_k)
        in_bias = jax.random.uniform(k3, (D_HID,), dtype=jnp.float32, minval=-init_k, maxval=init_k)
        out_weight = jax.random.uniform(k4, (D_HID, D_OUT), dtype=jnp.float32, minval=-init_k2, maxval=init_k2)
        return {'x': x, 'in_weight': in_weight, 'in_bias': in_bias, 'out_weight': out_weight}
    _L0_ffn_all = _L0_ffn_setup()
    _L0_ffn_in = {k: v for k, v in _L0_ffn_all.items() if k in ('in_weight', 'in_bias', 'out_weight')}
    del _L0_ffn_all
    return {'x': x, 'L0_tok_color_W': _L0_tok_in['color_W'], 'L0_tok_shape_W': _L0_tok_in['shape_W'], 'L0_tok_quantity_W': _L0_tok_in['quantity_W'], 'L0_tok_special_W': _L0_tok_in['special_W'], 'L0_attn_qkv_w': _L0_attn_in['qkv_w'], 'L0_attn_proj_w': _L0_attn_in['proj_w'], 'L0_attn_proj_b': _L0_attn_in['proj_b'], 'L0_attn_tab_kv': _L0_attn_in['tab_kv'], 'L0_attn_tab_kh': _L0_attn_in['tab_kh'], 'L0_attn_tab_vv': _L0_attn_in['tab_vv'], 'L0_attn_tab_vh': _L0_attn_in['tab_vh'], 'L0_ffn_in_weight': _L0_ffn_in['in_weight'], 'L0_ffn_in_bias': _L0_ffn_in['in_bias'], 'L0_ffn_out_weight': _L0_ffn_in['out_weight']}

def reference(x, L0_tok_color_W, L0_tok_shape_W, L0_tok_quantity_W, L0_tok_special_W, L0_attn_qkv_w, L0_attn_proj_w, L0_attn_proj_b, L0_attn_tab_kv, L0_attn_tab_kh, L0_attn_tab_vv, L0_attn_tab_vh, L0_ffn_in_weight, L0_ffn_in_bias, L0_ffn_out_weight):
    import jax
    import jax.numpy as jnp

    def _L0_tok_ref(tokens, color_W, shape_W, quantity_W, special_W):
        import jax, jax.numpy as jnp
        import numpy as np
        import math
        D_MODEL = 192
        BASE = D_MODEL // 3

        def positional_encoding(seq_length, d_model, dtype=jnp.float32):
            pos = jnp.arange(seq_length, dtype=dtype)[:, None]
            i_even = jnp.arange(0, d_model, 2, dtype=dtype)
            inv = jnp.exp(-(i_even / d_model) * math.log(10000.0))
            ang = pos * inv
            pe = jnp.stack([jnp.sin(ang), jnp.cos(ang)], axis=-1)
            return pe.reshape(seq_length, d_model)
        B, S = tokens.shape
        d_model = special_W.shape[1]
        t = jnp.minimum(tokens, 63)
        color = t // 16
        shape = t % 16 // 4
        quantity = t % 4
        feat_emb = jnp.concatenate([color_W[color], shape_W[shape], quantity_W[quantity]], axis=-1)
        sp_idx = jnp.clip(tokens - 64, 0, special_W.shape[0] - 1)
        spec_emb = special_W[sp_idx]
        emb = jnp.where((tokens < 64)[..., None], feat_emb, spec_emb)
        pe = positional_encoding(S, d_model, dtype=emb.dtype)
        out = emb * jnp.asarray(math.sqrt(d_model), emb.dtype) + pe[None, :, :]
        return out

    def _L0_attn_ref(x, qkv_w, proj_w, proj_b, tab_kv, tab_kh, tab_vv, tab_vh):
        import jax, jax.numpy as jnp
        import numpy as np
        B, N, DIM = (16, 577, 192)
        HEADS, HEAD_DIM = (12, 64)
        QKV_DIM = HEADS * HEAD_DIM
        MAX_REL = 14
        TABLE_ROWS = 2 * MAX_REL + 2

        def _rel_indices(n, max_rel):
            m = n - 1
            side = int(m ** 0.5)
            r = np.arange(m)
            dv = r[None, :] // side - r[:, None] // side
            dh = r[None, :] % side - r[:, None] % side
            iv = np.clip(dv, -max_rel, max_rel) + max_rel + 1
            ih = np.clip(dh, -max_rel, max_rel) + max_rel + 1
            iv = np.pad(iv, ((1, 0), (1, 0)))
            ih = np.pad(ih, ((1, 0), (1, 0)))
            return (jnp.asarray(iv), jnp.asarray(ih))
        b, n, _ = x.shape
        scale = HEAD_DIM ** (-0.5)
        qkv = (x @ qkv_w.T).reshape(b, n, 3, HEADS, HEAD_DIM).transpose(2, 0, 3, 1, 4)
        q, k, v = (qkv[0], qkv[1], qkv[2])
        attn = jnp.einsum('bhqd,bhkd->bhqk', q, k) * scale
        iv, ih = _rel_indices(n, MAX_REL)
        r_p_k = tab_kv[iv] + tab_kh[ih]
        attn = attn + jnp.einsum('bhqd,qkd->bhqk', q, r_p_k) * scale
        attn = jax.nn.softmax(attn, axis=-1)
        out = jnp.einsum('bhqk,bhkd->bhqd', attn, v)
        r_p_v = tab_vv[iv] + tab_vh[ih]
        out = out + jnp.einsum('bhqk,qkd->bhqd', attn, r_p_v)
        out = out.transpose(0, 2, 1, 3).reshape(b, n, QKV_DIM)
        return out @ proj_w.T + proj_b

    def _L0_ffn_ref(x, in_weight, in_bias, out_weight):
        import jax, jax.numpy as jnp
        import numpy as np
        B, S, D_IN, D_HID, D_OUT = (32, 128, 192, 768, 192)
        lead = x.shape[:-1]
        xt = x.reshape(-1, in_weight.shape[1])
        h = jax.nn.gelu(jnp.einsum('td,hd->th', xt, in_weight) + in_bias, approximate=False)
        out = jnp.einsum('th,ho->to', h, out_weight)
        return out.reshape(*lead, out_weight.shape[1])
    h = _L0_tok_ref(x, L0_tok_color_W, L0_tok_shape_W, L0_tok_quantity_W, L0_tok_special_W)
    h = h + _L0_attn_ref(_layernorm(h, axis=-1), L0_attn_qkv_w, L0_attn_proj_w, L0_attn_proj_b, L0_attn_tab_kv, L0_attn_tab_kh, L0_attn_tab_vv, L0_attn_tab_vh)
    h = h + _L0_ffn_ref(_layernorm(h, axis=-1), L0_ffn_in_weight, L0_ffn_in_bias, L0_ffn_out_weight)
    return h

_drawn_inputs = setup_inputs


def setup_inputs(seed=0):
    import zlib

    import numpy as np

    out = dict(_drawn_inputs(seed))
    spreads = {'L0_attn_proj_b': (0.0, 0.8)}
    factors = {'L0_attn_qkv_w': 8.0,
     'L0_attn_proj_w': 8.0,
     'L0_attn_tab_kv': 8.0,
     'L0_attn_tab_kh': 8.0,
     'L0_attn_tab_vv': 22.815,
     'L0_attn_tab_vh': 23.41,
     'L0_ffn_in_weight': 4.162,
     'L0_ffn_in_bias': 8.0,
     'L0_ffn_out_weight': 3.911}
    for name, (base, spread) in spreads.items():
        noise = np.random.default_rng([zlib.crc32(name.encode()), seed]).standard_normal(out[name].shape)
        drawn = base * np.exp(spread * noise) if base else spread * noise
        out[name] = jnp.asarray(drawn.astype(out[name].dtype))
    for name, factor in factors.items():
        out[name] = (out[name] * factor).astype(out[name].dtype)
    return out
```

```python
from contextlib import ExitStack
import math

import numpy as np
import concourse.bass as bass
from concourse import mybir

F32 = mybir.dt.float32
I32 = mybir.dt.int32
ALU = mybir.AluOpType
ACT = mybir.ActivationFunctionType
AX = mybir.AxisListType

B, S, D = 8, 256, 192
H, DH = 12, 64
PAIRS = H // 2
HID = 768
KC, KW = 2, D // 2
TC = S // 128
SIDE = int((S - 1) ** 0.5)
ROWS = (S - 1) // SIDE
MAX_REL = 14
REL = ROWS + SIDE
AUG = DH + REL
NGRP = ROWS + SIDE
VOCAB = 70
EPS = 1e-5
SCALE = DH ** -0.5
RPT, CPT = 5, 5
R_TILES = [range(g, min(g + RPT, ROWS)) for g in range(0, ROWS, RPT)]
C_TILES = [range(g, g + CPT) for g in range(0, SIDE, CPT)]
RN, CN = PAIRS * SIDE, PAIRS * ROWS
HTOK = S * B


def plan(with_tail, with_front):
    steps = [[] for _ in range(H)]
    def put(s, *tiles):
        steps[s] += tiles
    if with_tail:
        put(2, ("ow", 0))
        put(3, ("ow", 1), ("ow", 2))
        put(4, ("ow", 3), ("ow", 4))
        put(5, ("ow", 5))
        put(6, ("ra", 0), ("ra", 1))
        put(7, ("ra", 2))
        put(8, ("ra", 3))
        put(9, ("rc", 0), ("rc", 1))
        put(9, ("rc", 2))
        put(10, ("o", 0), ("o", 1))
    if with_front:
        put(0, ("q", 0), ("q", 1))
        put(1, ("q", 2), ("k", 0), ("k", 1))
        put(2, ("k", 2), ("a", 0), ("a", 1))
        put(3, ("a", 2))
        put(4, ("a", 3))
        put(5, ("b", 0))
        put(6, ("b", 1))
        put(7, ("b", 2))
        put(8, ("v", 0))
        put(9, ("v", 1))
        put(11, ("v", 2))
        put(11, ("v", 3))
    return steps


TILES = {"q": 3, "k": 3, "a": len(R_TILES), "b": len(C_TILES), "v": 4,
         "ow": PAIRS, "ra": len(R_TILES), "rc": len(C_TILES), "o": TC}
FRONT = ("q", "k", "a", "b", "v")
FRONT_DMAS = 8
ON_ACT = {"q", "ow", "v"}


class Batch:
    def __init__(self, k, i=None):
        self.k, self.i = k, i
        self.par = k % 2

    def at(self, n, c=0):
        if self.i is None:
            return n * self.k + c
        return self.i * (2 * n) + (n * self.k + c)

    def half(self, n, c=0):
        if self.i is None:
            return n * (self.k // 2) + c
        return self.i * n + (n * (self.k // 2) + c)

    def after(self, d):
        return Batch(self.k + d, self.i)

    def exists(self, d):
        return self.i is not None or 0 <= self.k + d < B


def wait(eng, sem, value):
    if not isinstance(value, int) or value > 0:
        eng.wait_ge(sem, value)


def build(nc, tok, etab, pe, qkw, proj_w, proj_b, key_rel, key_t0, val_rel, val_t0, key_hot, val_hot,
          ident_in, w1_in, b1_in, w2_in, out):
    with ExitStack() as ctx:
        def sb(name, shape, dt=F32):
            return ctx.enter_context(nc.sbuf_tensor(name, shape, dt))

        def sem(name):
            return ctx.enter_context(nc.semaphore(name))

        bank = [ctx.enter_context(nc.psum_tensor(f"bank{n}", [128, 512], F32)) for n in range(8)]
        score_bank, pt_bank, u_bank, g_bank = bank[0:2], bank[2:4], bank[4:6], bank[6:8]

        ident = sb("ident", [128, 128])
        etab_sb = sb("etab_sb", [VOCAB, D])
        iota_i = sb("iota_i", [128, 1], I32)
        iota_f = sb("iota_f", [128, 1])
        eps_sb = sb("eps_sb", [128, 1])
        wq_sb = sb("wq_sb", [KW, KC, 3 * H * DH])
        pw_sb = sb("pw_sb", [128, PAIRS, D])
        pb_sb = sb("pb_sb", [128, D])
        key_rel_sb = sb("key_rel_sb", [128, NGRP + 2, 64])
        val_rel_sb = sb("val_rel_sb", [64, NGRP + 1, 128])
        key_t0_sb = sb("key_t0_sb", [128, 2])
        key_t0s = sb("key_t0s", [128, 1])
        val_t0_sb = sb("val_t0_sb", [1, 2, DH])
        val_t0s = sb("val_t0s", [1, DH])
        b1_sb = sb("b1_sb", [128, HID // 128])
        h_sb = sb("h_sb", [128, B * TC, D])
        stats = sb("stats", [128, B * TC, 6])
        mv = sb("mv", [128, B * TC, 2])
        rstd = sb("rstd", [128, B * TC])
        xT = sb("xT", [KW, KC, HTOK])
        xb = [sb(f"xb{p}", [KW, KC, S]) for p in range(2)]
        q_pair = sb("q_pair", [128, PAIRS, S])
        k_pair = sb("k_pair", [128, PAIRS, S])
        ab_stage = sb("ab_stage", [128, PAIRS, S])
        a_stage, b_stage = ab_stage[0:64], ab_stage[64:128]
        Q = [sb(f"Q{p}", [AUG, H, S]) for p in range(2)]
        K = [sb(f"K{p}", [AUG, H, S]) for p in range(2)]
        V = [sb(f"V{p}", [128, TC, H, AUG]) for p in range(2)]
        tok_sb = Q[0][0:VOCAB].rearrange("p h s -> p (h s)")[:, 0:HTOK].bitcast(I32)
        onehot = Q[1][0:VOCAB].rearrange("p h s -> p (h s)")[:, 0:HTOK]
        negmax = sb("negmax", [128, 4, TC])
        den = sb("den", [128, PAIRS, 2, TC])
        rden = sb("rden", [128, PAIRS, 2, TC])
        P = [sb(f"P{p}", [128, TC, S]) for p in range(2)]
        PT = [sb(f"PT{p}", [128, TC, S]) for p in range(2)]
        On = [sb(f"On{p}", [128, TC, H, DH]) for p in range(2)]
        Wn = [sb(f"Wn{p}", [128, TC, H, REL]) for p in range(2)]
        OT = sb("OT", [128, PAIRS, S])
        WT = sb("WT", [64, PAIRS, S])
        hn = OT[:].rearrange("p r s -> p (r s)")[:, 0:2 * TC * D].rearrange("p (a t d) -> p a t d", a=2, t=TC)
        pe_sb = P[0][:].rearrange("p t s -> p (t s)")[:, 0:TC * D].rearrange("p (t d) -> p t d", t=TC)
        w1_sb = K[0][0:KW].rearrange("p h s -> p (h s)")[:, 0:KC * HID].rearrange("p (k n) -> p k n", k=KC)
        w2_sb = V[0][:].rearrange("p t h f -> p (t h f)")[:, 0:HID // 128 * D].rearrange("p (m n) -> p m n", n=D)
        gT = [t[:, :, :] for t in (q_pair, k_pair)]
        obuf = [t[:].rearrange("p t h f -> p (t h f)")[:, 0:TC * D].rearrange("p (t d) -> p t d", t=TC) for t in On]

        def load(name):
            return sem("ld_" + name)
        ld_tok, ld_emb, ld_w, ld_rel, ld_hot, ld_proj, ld_ffn = map(
            load, ("tok", "emb", "w", "rel", "hot", "proj", "ffn"))
        iota_done = sem("iota_done")
        iota_cast = sem("iota_cast")
        clamped = sem("clamped")
        onehot_ready = sem("onehot_ready")
        zeroed = sem("zeroed")
        eps_set = sem("eps_set")
        t0_ready = sem("t0_ready")
        emb_full = sem("emb_full")
        h_ready = sem("h_ready")
        stats_done = sem("stats_done")
        mv_done = sem("mv_done")
        std_done = sem("std_done")
        rstd_done = sem("rstd_done")
        hn_ready = sem("hn_ready")
        hn_turned = sem("hn_turned")
        xT_ready = sem("xT_ready")
        bias_added = sem("bias_added")
        x_ready = [sem(f"x_ready{p}") for p in range(2)]
        filled = {kind: sem("filled_" + kind) for kind in TILES}
        moved = {kind: sem("moved_" + kind) for kind in TILES}
        k_ready = sem("k_ready")
        v_ready = sem("v_ready")
        front_dma = sem("front_dma")
        scores_ready = sem("scores_ready")
        negmax_ready = sem("negmax_ready")
        probs_ready = sem("probs_ready")
        pt_full = sem("pt_full")
        pt_ready = sem("pt_ready")
        pv_done = sem("pv_done")
        rden_done = sem("rden_done")
        u_done = sem("u_done")
        f1_full = sem("f1_full")
        g_ready = sem("g_ready")
        f2_full = sem("f2_full")
        o_ready = [sem(f"o_ready{p}") for p in range(2)]
        o_sent = [sem(f"o_sent{p}") for p in range(2)]

        def in_order(b, steps, first, before):
            seq = list(before)
            out_steps = []
            for tl in steps:
                cur = []
                for kind, j in tl:
                    tb = b.after(1) if kind in FRONT else b.after(-1)
                    n = len(seq) - 2
                    cur.append((tb, kind, j, (first + n) % 2, seq[n]))
                    seq.append((tb, kind, j))
                out_steps.append(cur)
            return out_steps

        def last_two(b):
            return [(b, "v", TILES["v"] - 2), (b, "v", TILES["v"] - 1)]

        def tiles(b):
            static = b.i is None
            steps = plan(b.exists(-1), b.exists(1))
            if static and b.k == 0:
                return in_order(b, steps, FRONT_TILES, last_two(b))
            return in_order(b, steps, 0, last_two(b))

        FRONT_TILES = sum(TILES[k] for k in FRONT)
        first_front = in_order(Batch(-1), plan(False, True), 0, [None, None])
        last_tail = in_order(Batch(B), plan(True, False), sum(TILES.values()) - FRONT_TILES,
                             [(Batch(B - 2), "o", 0), (Batch(B - 2), "o", 1)])

        block = ctx.enter_context(nc.Block())

        @block.sync
        def _(sp):
            sp.dma_start(tok_sb, tok.rearrange("b s -> (b s)").partition_broadcast(VOCAB)).then_inc(ld_tok, 16)
            sp.dma_start(etab_sb[:], etab).then_inc(ld_emb, 16)
            sp.dma_start(pe_sb, pe.rearrange("(t p) d -> p t d", p=128)).then_inc(ld_emb, 16)
            sp.dma_start(wq_sb[:], qkw.rearrange("(c p) n -> p c n", p=KW)).then_inc(ld_w, 16)
            sp.wait_ge(zeroed, 2)
            for e in range(2):
                r = slice(64 * e, 64 * e + 64)
                sp.dma_start(key_rel_sb[r, :, 32 * e:32 * e + 32], key_rel).then_inc(ld_rel, 16)
                sp.dma_start(key_t0_sb[r, :], key_t0).then_inc(ld_rel, 16)
                sp.dma_start(val_rel_sb[32 * e:32 * e + 32, :, 64 * e:64 * e + 64], val_rel).then_inc(ld_rel, 16)
            sp.dma_start(val_t0_sb[:], val_t0.rearrange("(o a) d -> o a d", o=1)).then_inc(ld_rel, 16)

            def known(value):
                return value if isinstance(value, int) else sp.snap(value)

            def load_x(b):
                x_used = known(b.at(4, -4))
                src = xT[:, :, bass.ds(known(b.at(S)), S)]
                if b.i is None:
                    sp.wait_ge(xT_ready, b.k + 1)
                wait(sp, filled["v"], x_used)
                sp.dma_start(xb[b.par][:], src).then_inc(x_ready[b.par], 16)

            def place_front(b):
                qk_used = known(b.at(H, -H))
                ready = [known(b.at(n, n)) for n in (TILES["q"], 1, TILES["a"], TILES["b"])]
                wait(sp, scores_ready, qk_used)
                for src, dst, staged, n in ((q_pair, Q, moved["q"], ready[0]), (k_pair, K, k_ready, ready[1])):
                    sp.wait_ge(staged, n)
                    for e in range(2):
                        sp.dma_start(dst[b.par][0:DH, e::2, :], src[64 * e:64 * e + 64, :, :]).then_inc(front_dma, 16)
                for src, kind, r0, n, ev in ((a_stage, "a", DH, ROWS, ready[2]), (b_stage, "b", DH + ROWS, SIDE, ready[3])):
                    sp.wait_ge(moved[kind], ev)
                    for e in range(2):
                        sp.dma_start(Q[b.par][r0:r0 + n, e::2, :], src[32 * e:32 * e + n, :, :]).then_inc(front_dma, 16)

            load_x(Batch(0))
            load_x(Batch(1))
            sp.wait_ge(xT_ready, B)
            place_front(Batch(0))

            def batch(b):
                if b.exists(2):
                    load_x(b.after(2))
                if b.exists(1):
                    place_front(b.after(1))

            for k in range(B):
                batch(Batch(k))
            sp.wait_ge(scores_ready, H * (B - 1))
            sp.dma_start(w1_sb, w1_in.rearrange("(c p) n -> p c n", p=KW)).then_inc(ld_ffn, 16)
            sp.wait_ge(pv_done, H * (B - 1))
            sp.dma_start(w2_sb, w2_in.rearrange("(m p) n -> p m n", p=128)).then_inc(ld_ffn, 16)
            with sp.Fori(0, B // 2) as i:
                for p in range(2):
                    sent, at = known(i + 1), known(Batch(p, i).at(1))
                    sp.wait_ge(o_ready[p], sent)
                    sp.dma_start(out[bass.ds(at, 1), :, :].rearrange("b (t p) d -> p (b t) d", p=128),
                                 obuf[p]).then_inc(o_sent[p], 16)
            for p in range(2):
                sp.wait_ge(o_sent[p], 16 * (B // 2))

        @block.gpsimd
        def _(pool):
            pool.iota(iota_i[:], [[0, 1]], base=0, channel_multiplier=1).then_inc(iota_done, 1)
            pool.memset(key_rel_sb[:], 0.0).then_inc(zeroed, 1)
            pool.memset(val_rel_sb[:], 0.0).then_inc(zeroed, 1)
            pool.wait_ge(ld_proj, 32)
            for t in range(B):
                pool.wait_ge(hn_ready, t + 1)
                pool.tensor_tensor(h_sb[:, TC * t:TC * t + TC, :], h_sb[:, TC * t:TC * t + TC, :],
                                   pb_sb[:].unsqueeze(1).to_broadcast([128, TC, D]), ALU.add).then_inc(bias_added, 1)

        def evacuate(eng, on_act, b, kind, j, bk):
            G = g_bank[bk]
            p = b.par
            eng.wait_ge(filled[kind], b.at(TILES[kind], j + 1))

            def copy(dst, src, scale=1.0):
                if on_act:
                    return eng.activation(dst, src, ACT.Copy, scale=scale)
                if scale != 1.0:
                    return eng.tensor_scalar(dst, src, scale, None, ALU.mult)
                return eng.tensor_copy(dst, src)

            if j == 0 and kind in ("q", "k", "a", "b"):
                wait(eng, front_dma, b.at(16 * FRONT_DMAS))
            if j == 0 and kind == "v":
                wait(eng, pv_done, b.at(H, -H))
            if j == 0 and kind == "ow":
                if b.exists(1):
                    eng.wait_ge(filled["v"], b.at(4, 8))
                else:
                    eng.wait_ge(filled["o"], b.at(TC))
            if kind == "ra" and j == 0:
                eng.wait_ge(moved["ow"], b.at(PAIRS, PAIRS))
            if kind == "rc" and j == 0:
                eng.wait_ge(moved["ra"], b.at(TILES["ra"], TILES["ra"]))

            if kind in ("q", "k"):
                dst = {"q": q_pair, "k": k_pair}[kind]
                ins = copy(dst[:, 2 * j:2 * j + 2, :], G[:, :].rearrange("p (r s) -> p r s", r=2),
                           SCALE if kind == "q" else 1.0)
            elif kind == "ow":
                copy(OT[:, j, :], G[:, 0:S])
                ins = copy(WT[:, j, :], G[0:64, S:2 * S])
            elif kind == "v":
                ins = copy(V[p][:, j // 2, 6 * (j % 2):6 * (j % 2) + 6, 0:DH],
                           G[:, 0:6 * DH].rearrange("p (h d) -> p h d", h=6))
            elif kind == "o":
                o = h_sb[:, bass.ds(b.at(TC, j), 1), :]
                ins = eng.tensor_tensor(o, G[:, 0:D].unsqueeze(1), o, ALU.add)
            elif kind in ("a", "ra"):
                g = R_TILES[j]
                n = len(g)
                dst, src = (a_stage, G[0:64]) if kind == "a" else (OT[:], G[:])
                dst_g = dst[:, :, 1 + SIDE * g[0]:1 + SIDE * (g[0] + n)].rearrange("p r (g c) -> p r g c", g=n)
                src_g = src[:, 0:n * RN].rearrange("p (g r c) -> p r g c", g=n, r=PAIRS)
                ins = copy(dst_g, src_g) if kind == "a" else eng.tensor_tensor(dst_g, src_g, dst_g, ALU.add)
                if j == len(R_TILES) - 1:
                    c0 = n * RN
                    if kind == "a":
                        copy(a_stage[:, :, 0], G[0:64, c0:c0 + PAIRS])
                        ins = copy(b_stage[:, :, 0], G[64:128, c0 + PAIRS:c0 + 2 * PAIRS])
                    else:
                        ins = eng.tensor_tensor(OT[:, :, 0], G[:, c0:c0 + PAIRS], OT[:, :, 0], ALU.add)
            elif kind in ("b", "rc"):
                g = C_TILES[j]
                dst, src = (b_stage, G[64:128]) if kind == "b" else (OT[:], G[:])
                dst_g = dst[:, :, 1:S].rearrange("p r (a c) -> p r c a", c=SIDE)[:, :, g[0]:g[0] + CPT, :]
                src_g = src[:, 0:CPT * CN].rearrange("p (c r a) -> p r c a", c=CPT, r=PAIRS)
                ins = copy(dst_g, src_g) if kind == "b" else eng.tensor_tensor(dst_g, src_g, dst_g, ALU.add)
            ins.then_inc(moved[kind], 1)

        @block.scalar
        def _(act):
            act.dma_start(ident[:], ident_in).then_inc(ld_emb, 16)
            act.dma_start(pw_sb[:], proj_w.rearrange("(r p) n -> p r n", p=128)).then_inc(ld_proj, 16)
            act.dma_start(pb_sb[:], proj_b.partition_broadcast(128)).then_inc(ld_proj, 16)
            for p in range(2):
                act.dma_start(K[p][DH:AUG, :, :], key_hot.unsqueeze(1).to_broadcast([REL, H, S])).then_inc(ld_hot, 16)
                for t in range(TC):
                    act.dma_start(V[p][:, t, :, DH:AUG],
                                  val_hot[128 * t:128 * t + 128, :].unsqueeze(1).to_broadcast([128, H, REL])).then_inc(ld_hot, 16)
            act.dma_start(b1_sb[:], b1_in).then_inc(ld_ffn, 16)

            def std(r):
                act.wait_ge(mv_done, r * B * TC)
                act.activation(rstd[:], mv[:, :, 1], ACT.Sqrt, bias=eps_sb[:, 0:1]).then_inc(std_done, 1)

            act.wait_ge(eps_set, 1)
            std(1)

            def exps(b, h):
                act.wait_ge(negmax_ready, b.at(H, h + 1))
                wait(act, pt_full, b.at(H, h - 1))
                for t in range(TC):
                    ins = act.activation(P[h % 2][:, t, :], score_bank[h % 2][:, t * S:t * S + S], ACT.Exp,
                                         bias=negmax[:, h % 4, t:t + 1],
                                         accum_out=den[:, h // 2, h % 2, t:t + 1])
                ins.then_inc(probs_ready, 1)

            def move_pt(b, h):
                act.wait_ge(pt_full, b.at(H, h + 1))
                wait(act, pv_done, b.at(H, h - 1))
                act.activation(PT[h % 2][:], pt_bank[h % 2][:, :].rearrange("p (k q) -> p k q", k=TC),
                               ACT.Copy).then_inc(pt_ready, 1)

            def side(tl):
                for tb, kind, j, bk, _ in tl:
                    if kind in ON_ACT:
                        evacuate(act, True, tb, kind, j, bk)

            def batch(b):
                for s, tl in enumerate(tiles(b)):
                    exps(b, s)
                    if s >= 1:
                        move_pt(b, s - 1)
                    elif b.exists(-1):
                        move_pt(b.after(-1), H - 1)
                    side(tl)

            for tl in first_front:
                side(tl)
            batch(Batch(0))
            with act.Fori(0, (B - 2) // 2) as i:
                batch(Batch(1, i))
                batch(Batch(2, i))
            batch(Batch(B - 1))
            move_pt(Batch(B - 1), H - 1)
            for tl in last_tail:
                side(tl)

            std(2)
            act.wait_ge(ld_ffn, 48)

            def gelus(b):
                wait(act, f2_full, b.at(1, -1))
                for m in range(HID // 128):
                    if m % 2 == 0:
                        act.wait_ge(f1_full, b.at(3, m // 2 + 1))
                    act.activation(gT[b.par][:, m, :], bank[3 * b.par + m // 2][:, (m % 2) * S:(m % 2) * S + S],
                                   ACT.Gelu, bias=b1_sb[:, m:m + 1]).then_inc(g_ready, 1)

            for p in range(2):
                gelus(Batch(p))
            with act.Fori(0, B // 2 - 1) as i:
                for p in range(2):
                    gelus(Batch(2 + p, i))

        @block.vector
        def _(dve):
            dve.memset(eps_sb[:], EPS).then_inc(eps_set, 1)
            dve.wait_ge(iota_done, 1)
            dve.tensor_copy(iota_f[:], iota_i[:]).then_inc(iota_cast, 1)
            dve.wait_ge(iota_cast, 1)
            dve.wait_ge(ld_tok, 16)
            for c in range(B):
                dve.tensor_scalar(onehot[:, c * S:c * S + S], tok_sb[:, c * S:c * S + S], float(VOCAB - 1),
                                  iota_f[0:VOCAB, 0:1], ALU.min, ALU.is_equal).then_inc(onehot_ready, 1)
            dve.wait_ge(ld_emb, 48)
            for c in range(B):
                dve.wait_ge(emb_full, c + 1)
                dve.scalar_tensor_tensor(out=h_sb[:, TC * c:TC * c + TC, :].rearrange("p t d -> p (t d)"),
                                         in0=bank[c][:, 0:TC * D], scalar=math.sqrt(D),
                                         in1=pe_sb.rearrange("p t d -> p (t d)"),
                                         op0=ALU.mult, op1=ALU.add).then_inc(h_ready, 1)

            def moments(r):
                for t in range(B * TC):
                    if r == 1:
                        dve.wait_ge(h_ready, t // TC + 1)
                    else:
                        dve.wait_ge(moved["o"], t + 1)
                    dve.bn_stats(stats[:, t, :], h_sb[:, t, :]).then_inc(stats_done, 1)
                for t in range(B * TC):
                    dve.wait_ge(stats_done, (r - 1) * B * TC + t + 1)
                    dve.bn_aggr(mv[:, t, :], stats[:, t, :]).then_inc(mv_done, 1)
                dve.wait_ge(std_done, r)
                dve.reciprocal(rstd[:], rstd[:]).then_inc(rstd_done, 1)
                dve.wait_ge(rstd_done, r)

            def normalise(r):
                def out_xT(c):
                    dve.wait_ge(hn_turned, (r - 1) * B + c + 1)
                    dve.tensor_copy(xT[:, :, c * S:c * S + S],
                                    bank[c][0:KW, :].rearrange("p (k s) -> p k s", k=KC)).then_inc(xT_ready, 1)
                for c in range(B):
                    if c >= 2:
                        dve.wait_ge(hn_turned, (r - 1) * B + c - 1)
                    for t in range(TC):
                        n = TC * c + t
                        ins = dve.tensor_scalar(hn[:, c % 2, t, :], h_sb[:, n, :], mv[:, n, 0:1], rstd[:, n:n + 1],
                                                ALU.subtract, ALU.mult)
                    ins.then_inc(hn_ready, 1)
                    if c >= 1:
                        out_xT(c - 1)
                out_xT(B - 1)

            moments(1)
            normalise(1)
            dve.wait_ge(ld_rel, 16 * 7)
            dve.tensor_tensor(key_t0s[:], key_t0_sb[:, 0:1], key_t0_sb[:, 1:2], ALU.add).then_inc(t0_ready, 1)
            dve.tensor_tensor(val_t0s[:], val_t0_sb[:, 0, :], val_t0_sb[:, 1, :], ALU.add).then_inc(t0_ready, 1)
            dve.wait_ge(t0_ready, 2)
            dve.wait_ge(bias_added, B)

            def maxima(b, h):
                dve.wait_ge(scores_ready, b.at(H, h + 1))
                dve.tensor_reduce(negmax[:, h % 4, :], score_bank[h % 2][:, :].rearrange("p (t s) -> p t s", t=TC),
                                  AX.X, ALU.max, negate=True).then_inc(negmax_ready, 1)

            def normalise_u(b, pr):
                if pr == 0:
                    dve.wait_ge(filled["v"], b.at(4, 4))
                dve.wait_ge(probs_ready, b.at(H, 2 * pr + 2))
                dve.reciprocal(rden[:, pr, :, :], den[:, pr, :, :]).then_inc(rden_done, 1)
                dve.wait_ge(rden_done, b.at(PAIRS, pr + 1))
                dve.wait_ge(pv_done, b.at(H, 2 * pr + 2))
                U = u_bank[pr % 2][:, 0:2 * TC * AUG].rearrange("p (e t f) -> p e t f", e=2, t=TC)
                for dst, c0, w in ((On, 0, DH), (Wn, DH, REL)):
                    ins = dve.tensor_tensor(
                        dst[b.par][:, :, 2 * pr:2 * pr + 2, :].rearrange("p t e f -> p e t f"),
                        U[:, :, :, c0:c0 + w],
                        rden[:, pr, :, :].unsqueeze(3).to_broadcast([128, 2, TC, w]), ALU.mult)
                ins.then_inc(u_done, 1)

            def side(tl):
                for tb, kind, j, bk, _ in tl:
                    if kind not in ON_ACT:
                        evacuate(dve, False, tb, kind, j, bk)
                    if kind == "k" and j == PAIRS // 2 - 1:
                        dve.wait_ge(moved["k"], tb.at(TILES["k"], TILES["k"]))
                        dve.tensor_scalar(k_pair[:, :, 0], k_pair[:, :, 0], key_t0s[:, 0:1], None,
                                          ALU.add).then_inc(k_ready, 1)
                    if kind == "v" and j == 3:
                        dve.wait_ge(moved["v"], tb.at(4, 4))
                        v0 = V[tb.par][0:1, 0, :, 0:DH]
                        dve.tensor_tensor(v0, v0, val_t0s[0:1, :].unsqueeze(1).to_broadcast([1, H, DH]),
                                          ALU.add).then_inc(v_ready, 1)

            def batch(b):
                for s, tl in enumerate(tiles(b)):
                    maxima(b, s)
                    if s >= 3 and s % 2 == 1:
                        normalise_u(b, (s - 3) // 2)
                    elif s == 1 and b.exists(-1):
                        normalise_u(b.after(-1), PAIRS - 1)
                    side(tl)

            for tl in first_front:
                side(tl)
            batch(Batch(0))
            with dve.Fori(0, (B - 2) // 2) as i:
                batch(Batch(1, i))
                batch(Batch(2, i))
            batch(Batch(B - 1))
            normalise_u(Batch(B - 1), PAIRS - 1)
            for tl in last_tail:
                side(tl)

            moments(2)
            normalise(2)
            def results(b):
                p = b.par
                dve.wait_ge(f2_full, b.at(1, 1))
                wait(dve, o_sent[p], b.half(16))
                dve.tensor_tensor(obuf[p], bank[6 + p][:, 0:TC * D].rearrange("p (t d) -> p t d", t=TC),
                                  h_sb[:, bass.ds(b.at(TC), TC), :], ALU.add).then_inc(o_ready[p], 1)

            for p in range(2):
                results(Batch(p))
            with dve.Fori(0, B // 2 - 1) as i:
                for p in range(2):
                    results(Batch(2 + p, i))

        @block.tensor
        def _(pe_):
            mm = pe_.matmul
            pe_.wait_ge(ld_emb, 48)
            for c in range(B):
                pe_.wait_ge(onehot_ready, c + 1)
                for t in range(TC):
                    n = TC * c + t
                    ins = mm(bank[c][:, t * D:t * D + D], onehot[:, n * 128:n * 128 + 128], etab_sb[:],
                             start=True, stop=True)
                ins.then_inc(emb_full, 1)

            def turn_hn(r):
                for c in range(B):
                    pe_.wait_ge(hn_ready, (r - 1) * B + c + 1)
                    for k in range(KC):
                        for t in range(TC):
                            ins = pe_.transpose(bank[c][0:KW, k * S + t * 128:k * S + t * 128 + 128],
                                                hn[:, c % 2, t, k * KW:k * KW + KW], ident[:])
                    ins.then_inc(hn_turned, 1)

            turn_hn(1)
            pe_.wait_ge(xT_ready, B)
            pe_.wait_ge(ld_w, 16)
            pe_.wait_ge(ld_rel, 16 * 7)
            pe_.wait_ge(ld_hot, 16 * 2 * (1 + TC))
            pe_.wait_ge(ld_proj, 32)

            def scores(b, h):
                if h == 0:
                    pe_.wait_ge(front_dma, b.at(16 * FRONT_DMAS, 16 * FRONT_DMAS))
                wait(pe_, probs_ready, b.at(H, h - 1))
                for t in range(TC):
                    ins = mm(score_bank[h % 2][:, t * S:t * S + S], Q[b.par][:, h, t * 128:t * 128 + 128],
                             K[b.par][:, h, :], start=True, stop=True)
                ins.then_inc(scores_ready, 1)

            def turn_p(b, h):
                pe_.wait_ge(probs_ready, b.at(H, h + 1))
                wait(pe_, pt_ready, b.at(H, h - 1))
                for k in range(TC):
                    for t in range(TC):
                        ins = pe_.transpose(pt_bank[h % 2][:, k * S + t * 128:k * S + t * 128 + 128],
                                            P[h % 2][:, t, k * 128:k * 128 + 128], ident[:])
                ins.then_inc(pt_full, 1)

            def values(b, h):
                if h == 0:
                    pe_.wait_ge(v_ready, b.at(1, 1))
                if h % 2 == 0:
                    wait(pe_, u_done, b.at(PAIRS, h // 2 - 1))
                pe_.wait_ge(pt_ready, b.at(H, h + 1))
                for t in range(TC):
                    for k in range(TC):
                        c0 = (TC * (h % 2) + t) * AUG
                        ins = mm(u_bank[(h // 2) % 2][:, c0:c0 + AUG], PT[h % 2][:, k, t * 128:t * 128 + 128],
                                 V[b.par][:, k, h, :], start=(k == 0), stop=(k == TC - 1))
                ins.then_inc(pv_done, 1)

            def fill(b, kind, j, bk, before):
                G = g_bank[bk]
                if before is not None:
                    b0, kind0, j0 = before
                    wait(pe_, moved[kind0], b0.at(TILES[kind0], j0 + 1))
                p = b.par
                if kind in "qk":
                    if kind == "q" and j == 0:
                        pe_.wait_ge(x_ready[p], b.half(16, 16))
                    for r in range(2):
                        n0 = (0 if kind == "q" else H * DH) + (2 * j + r) * 128
                        for k in range(KC):
                            ins = mm(G[:, r * S:r * S + S], wq_sb[:, k, n0:n0 + 128], xb[p][:, k, :],
                                     start=(k == 0), stop=(k == KC - 1))
                elif kind == "v":
                    for k in range(KC):
                        n0 = 2 * H * DH + (j % 2) * 6 * DH
                        ins = mm(G[:, 0:6 * DH], xb[p][:, k, (j // 2) * 128:(j // 2) * 128 + 128],
                                 wq_sb[:, k, n0:n0 + 6 * DH], start=(k == 0), stop=(k == KC - 1))
                elif kind == "a":
                    if j == 0:
                        pe_.wait_ge(moved["q"], b.at(3, 3))
                    for m, g in enumerate(R_TILES[j]):
                        ins = mm(G[0:64, m * RN:m * RN + RN], key_rel_sb[:, g, :],
                                 q_pair[:, :, 1 + SIDE * g:1 + SIDE * g + SIDE], start=True, stop=True)
                    if j == len(R_TILES) - 1:
                        for m in range(2):
                            c0 = len(R_TILES[j]) * RN + m * PAIRS
                            ins = mm(G[64 * m:64 * m + 64, c0:c0 + PAIRS], key_rel_sb[:, NGRP + m, :], q_pair[:, :, 0],
                                     start=True, stop=True)
                elif kind == "b":
                    for m, g in enumerate(C_TILES[j]):
                        ins = mm(G[64:128, m * CN:m * CN + CN], key_rel_sb[:, ROWS + g, :],
                                 q_pair[:, :, 1 + g:S:SIDE], start=True, stop=True)
                elif kind == "ow":
                    if j == 0:
                        pe_.wait_ge(u_done, b.at(PAIRS, PAIRS))
                    for part, out_t in ((On, G[:, 0:S]), (Wn, G[0:64, S:2 * S])):
                        for t in range(TC):
                            ins = pe_.transpose(out_t[:, t * 128:t * 128 + 128],
                                                part[p][:, t, 2 * j:2 * j + 2, :].rearrange("p e f -> p (e f)"), ident[:])
                elif kind == "ra":
                    if j == 0:
                        pe_.wait_ge(moved["ow"], b.at(PAIRS, PAIRS))
                    for m, g in enumerate(R_TILES[j]):
                        ins = mm(G[:, m * RN:m * RN + RN], val_rel_sb[:, g, :],
                                 WT[:, :, 1 + SIDE * g:1 + SIDE * g + SIDE], start=True, stop=True)
                    if j == len(R_TILES) - 1:
                        c0 = len(R_TILES[j]) * RN
                        ins = mm(G[:, c0:c0 + PAIRS], val_rel_sb[:, NGRP, :], WT[:, :, 0], start=True, stop=True)
                elif kind == "rc":
                    for m, g in enumerate(C_TILES[j]):
                        ins = mm(G[:, m * CN:m * CN + CN], val_rel_sb[:, ROWS + g, :],
                                 WT[:, :, 1 + g:S:SIDE], start=True, stop=True)
                elif kind == "o":
                    if j == 0:
                        pe_.wait_ge(moved["rc"], b.at(3, 3))
                    for r in range(PAIRS):
                        ins = mm(G[:, 0:D], OT[:, r, j * 128:j * 128 + 128], pw_sb[:, r, :],
                                 start=(r == 0), stop=(r == PAIRS - 1))
                ins.then_inc(filled[kind], 1)

            def side(tl):
                for tile in tl:
                    fill(*tile)

            def batch(b):
                for s, tl in enumerate(tiles(b)):
                    scores(b, s)
                    if s >= 1:
                        turn_p(b, s - 1)
                    elif b.exists(-1):
                        turn_p(b.after(-1), H - 1)
                    if s >= 2:
                        values(b, s - 2)
                    elif b.exists(-1):
                        values(b.after(-1), H - 2 + s)
                    side(tl)

            for tl in first_front:
                side(tl)
            batch(Batch(0))
            with pe_.Fori(0, (B - 2) // 2) as i:
                batch(Batch(1, i))
                batch(Batch(2, i))
            batch(Batch(B - 1))
            turn_p(Batch(B - 1), H - 1)
            for h in (H - 2, H - 1):
                values(Batch(B - 1), h)
            for tl in last_tail:
                side(tl)

            turn_hn(2)
            pe_.wait_ge(xT_ready, 2 * B)
            pe_.wait_ge(ld_ffn, 48)

            def hidden(b):
                wait(pe_, g_ready, b.at(6, -6))
                for m in range(HID // 128):
                    for k in range(KC):
                        ins = mm(bank[3 * b.par + m // 2][:, (m % 2) * S:(m % 2) * S + S],
                                 w1_sb[:, k, m * 128:m * 128 + 128], xT[:, k, bass.ds(b.at(S), S)],
                                 start=(k == 0), stop=(k == KC - 1))
                    if m % 2 == 1:
                        ins.then_inc(f1_full, 1)

            def outputs(b):
                pe_.wait_ge(g_ready, b.at(6, 6))
                wait(pe_, o_ready[b.par], b.half(1))
                for t in range(TC):
                    for m in range(HID // 128):
                        ins = mm(bank[6 + b.par][:, t * D:t * D + D], gT[b.par][:, m, t * 128:t * 128 + 128],
                                 w2_sb[:, m, :], start=(m == 0), stop=(m == HID // 128 - 1))
                ins.then_inc(f2_full, 1)

            for p in range(2):
                hidden(Batch(p))
            for p in range(2):
                outputs(Batch(p))
                hidden(Batch(2 + p))
            with pe_.Fori(0, B // 2 - 2) as i:
                for p in range(2):
                    outputs(Batch(2 + p, i))
                    hidden(Batch(4 + p, i))
            for k in (B - 2, B - 1):
                outputs(Batch(k))


def rel_windows(table, n):
    q, k = np.arange(n)[:, None], np.arange(n)[None, :]
    return table[np.clip(k - q, -MAX_REL, MAX_REL) + MAX_REL + 1]


def kernel(**inputs):
    import concourse.bacc as bacc
    from concourse.bass_utils import run_bass_kernel_spmd

    a = {k.split("_", 2)[-1] if k.startswith("L0_") else k: np.asarray(v) for k, v in inputs.items()}
    code = np.arange(VOCAB - a["special_W"].shape[0])
    etab = np.concatenate([
        np.concatenate([a["color_W"][code // 16], a["shape_W"][code % 16 // 4], a["quantity_W"][code % 4]], axis=-1),
        a["special_W"]])
    even = np.arange(0, D, 2, dtype=np.float32)
    angle = np.arange(S, dtype=np.float32)[:, None] * np.exp(-(even / np.float32(D)) * np.float32(math.log(10000.0)))
    pe = np.stack([np.sin(angle), np.cos(angle)], axis=-1).reshape(S, D).astype(np.float32)

    key_rel = np.zeros((NGRP + 2, REL, DH), np.float32)
    key_rel[:ROWS, :ROWS] = rel_windows(a["tab_kv"], ROWS)
    key_rel[ROWS:NGRP, :SIDE] = rel_windows(a["tab_kh"], SIDE)
    key_rel[NGRP, :ROWS] = a["tab_kv"][0]
    key_rel[NGRP + 1, :SIDE] = a["tab_kh"][0]
    val_rel = np.zeros((NGRP + 1, REL, DH), np.float32)
    val_rel[:ROWS, :ROWS] = rel_windows(a["tab_vv"], ROWS)
    val_rel[ROWS:NGRP, ROWS:] = rel_windows(a["tab_vh"], SIDE)
    val_rel[NGRP, :ROWS] = a["tab_vv"][0]
    val_rel[NGRP, ROWS:] = a["tab_vh"][0]
    token = np.arange(1, S)
    hot = np.zeros((S, REL), np.float32)
    hot[token, (token - 1) // SIDE] = 1.0
    hot[token, ROWS + (token - 1) % SIDE] = 1.0

    arrays = {
        "tok": a["x"],
        "etab": etab,
        "pe": pe,
        "qkw": a["qkv_w"].T,
        "proj_w": a["proj_w"].T,
        "proj_b": a["proj_b"],
        "key_rel": key_rel.transpose(2, 0, 1),
        "key_t0": np.stack([a["tab_kv"][0], a["tab_kh"][0]], axis=1),
        "val_rel": val_rel.transpose(1, 0, 2),
        "val_t0": np.stack([a["tab_vv"][0], a["tab_vh"][0]]),
        "key_hot": hot.T,
        "val_hot": hot,
        "ident": np.eye(128, dtype=np.float32),
        "w1": a["in_weight"].T,
        "b1": a["in_bias"].reshape(HID // 128, 128).T,
        "w2": a["out_weight"],
    }
    nc = bacc.Bacc("TRN2", target_bir_lowering=False, num_devices=1)
    arrays = {k: np.ascontiguousarray(v) for k, v in arrays.items()}
    args = [nc.dram_tensor("in_" + k, v.shape, mybir.dt.from_np(v.dtype), kind="ExternalInput").ap()
            for k, v in arrays.items()]
    args.append(nc.dram_tensor("out", (B, S, D), F32, kind="ExternalOutput").ap())
    build(nc, *args)
    r = run_bass_kernel_spmd(nc, [{"in_" + k: v for k, v in arrays.items()}], core_ids=[0])
    return r.results[0]["out"]
```

```python
from contextlib import ExitStack
import math

import numpy as np
import concourse.bass as bass
from concourse import mybir

F32 = mybir.dt.float32
F32R = mybir.dt.float32r
I32 = mybir.dt.int32
ALU = mybir.AluOpType
ACT = mybir.ActivationFunctionType
AX = mybir.AxisListType

B, S, D = 8, 256, 192
H, DH = 12, 64
PAIRS = H // 2
HID = 768
DA, DB = 128, D - 128
TC = S // 128
SIDE = int((S - 1) ** 0.5)
ROWS = (S - 1) // SIDE
MAX_REL = 14
REL = ROWS + SIDE
AUG = DH + REL
NGRP = ROWS + SIDE
VOCAB = 70
EPS = 1e-5
SCALE = DH ** -0.5
RPT, CPT = 5, 5
R_TILES = [range(g, min(g + RPT, ROWS)) for g in range(0, ROWS, RPT)]
C_TILES = [range(g, g + CPT) for g in range(0, SIDE, CPT)]
RN, CN = PAIRS * SIDE, PAIRS * ROWS
NTOK = S * B
CHUNK = 1152


def plan(with_tail, with_front):
    steps = [[] for _ in range(H)]
    def put(s, *tiles):
        steps[s] += tiles
    if with_tail:
        put(2, ("ow", 0))
        put(3, ("ow", 1), ("ow", 2))
        put(4, ("ow", 3), ("ow", 4))
        put(5, ("ow", 5))
        put(6, ("ra", 0), ("ra", 1))
        put(7, ("ra", 2), ("ra", 3))
        put(8, ("rc", 0), ("rc", 1))
        put(9, ("rc", 2))
        put(10, ("o", 0))
    if with_front:
        put(0, ("x", 0))
        put(1, ("k", 0), ("k", 1))
        put(2, ("k", 2), ("q", 0))
        put(3, ("q", 1))
        put(4, ("q", 2))
        put(5, ("a", 0), ("a", 1))
        put(6, ("a", 2), ("a", 3))
        put(7, ("b", 0))
        put(8, ("b", 1), ("b", 2))
        put(9, ("v", 0))
        put(10, ("v", 1))
        put(11, ("v", 2), ("v", 3))
    return steps


TILES = {"x": 1, "q": 3, "k": 3, "a": len(R_TILES), "b": len(C_TILES), "v": 4,
         "ow": PAIRS, "ra": len(R_TILES), "rc": len(C_TILES), "o": 1}
FRONT = ("x", "q", "k", "a", "b", "v")
FRONT_DMAS = 6
G_BANKS = 4
ON_ACT = {"x", "q", "ow", "v"}
ON_DVE = {"x", "k", "a", "b", "ow", "ra", "rc", "o"}


class Batch:
    def __init__(self, k, i=None):
        self.k, self.i = k, i
        self.par = k % 2

    def at(self, n, c=0):
        if self.i is None:
            return n * self.k + c
        return self.i * (2 * n) + (n * self.k + c)

    def half(self, n, c=0):
        if self.i is None:
            return n * (self.k // 2) + c
        return self.i * n + (n * (self.k // 2) + c)

    def after(self, d):
        return Batch(self.k + d, self.i)

    def exists(self, d):
        return self.i is not None or 0 <= self.k + d < B


def wait(eng, sem, value):
    if not isinstance(value, int) or value > 0:
        eng.wait_ge(sem, value)


def high_low(eng, low, whole, high):
    return eng.tensor_tensor(low, whole, high.bitcast(F32), ALU.subtract)


def build(nc, tok, etab, pe, qkw, proj_w, proj_b, key_rel, key_t0, val_rel, val_t0, key_hot, val_hot,
          ident_in, w1_in, b1_in, w2_in, out):
    with ExitStack() as ctx:
        def sb(name, shape, dt=F32):
            return ctx.enter_context(nc.sbuf_tensor(name, shape, dt))

        def sem(name):
            return ctx.enter_context(nc.semaphore(name))

        bank = [ctx.enter_context(nc.psum_tensor(f"bank{n}", [128, 512], F32)) for n in range(8)]
        score_bank, pt_bank, u_bank, g_bank = bank[0:2], bank[2], bank[3], bank[4:8]

        ident = sb("ident", [128, 128])
        iota_i = sb("iota_i", [128, 1], I32)
        iota_f = sb("iota_f", [128, 1])
        eps_sb = sb("eps_sb", [128, 1])
        wa_hi = sb("wa_hi", [DA, 3 * H * DH], F32R)
        wa_lo = sb("wa_lo", [DA, 3 * H * DH], F32R)
        wb_hi = sb("wb_hi", [2 * DB, 3 * H * DH], F32R)
        lows = sb("lows", [128, (NGRP + 1) * 128], F32R)
        wb_lo, val_lo = lows[0:DB], lows[DB:128]
        pw_sb = sb("pw_sb", [128, PAIRS, D])
        pb_sb = sb("pb_sb", [128, D])
        key_rel_sb = sb("key_rel_sb", [128, NGRP + 2, 64])
        val_hi = sb("val_hi", [128, (NGRP + 1) * 128], F32R)
        key_t0_sb = sb("key_t0_sb", [128, 2])
        key_t0s = sb("key_t0s", [128, 1])
        val_t0_sb = sb("val_t0_sb", [1, 2, DH])
        val_t0s = sb("val_t0s", [1, DH])
        b1_sb = sb("b1_sb", [128, HID // 128])
        h_sb = sb("h_sb", [128, B * TC, D])
        stats = sb("stats", [128, B * TC, 6])
        mv = sb("mv", [128, B * TC, 2])
        rstd = sb("rstd", [128, B * TC])
        hn = sb("hn", [128, TC, D])
        x_hi = sb("x_hi", [128, 2, S], F32R)
        x_lo = sb("x_lo", [DA, S], F32R)
        q_pair = sb("q_pair", [128, PAIRS, S])
        k_pair = sb("k_pair", [128, PAIRS, S])
        a_stage, b_stage = k_pair[0:64], k_pair[64:128]
        Q = [sb(f"Q{p}", [AUG, H, S]) for p in range(2)]
        K = [sb(f"K{p}", [AUG, H, S]) for p in range(2)]
        V = [sb(f"V{p}", [128, TC, H, AUG]) for p in range(2)]
        tok_sb = Q[0][0:VOCAB].rearrange("p h s -> p (h s)")[:, 0:NTOK].bitcast(I32)
        onehot = Q[1][0:VOCAB].rearrange("p h s -> p (h s)")[:, 0:NTOK]
        negmax = sb("negmax", [128, 4, TC])
        den = sb("den", [128, PAIRS, 2, TC])
        rden = sb("rden", [128, PAIRS, 2, TC])
        P = [sb(f"P{p}", [128, TC, S]) for p in range(2)]
        PT = [sb(f"PT{p}", [128, TC, S]) for p in range(2)]
        On = sb("On", [128, TC, H, DH])
        Wn = sb("Wn", [128, TC, PAIRS, 2, 2, REL])
        OT = sb("OT", [128, PAIRS, S])
        WT = sb("WT", [128, PAIRS, S], F32R)
        etab_sb = PT[0][0:VOCAB].rearrange("p t s -> p (t s)")[:, 0:D]
        pe_sb = P[0][:].rearrange("p t s -> p (t s)")[:, 0:TC * D].rearrange("p (t d) -> p t d", t=TC)
        raw = [t[:].rearrange("p t h f -> p (t h f)")[:, c:c + CHUNK] for t in V for c in (0, CHUNK)]
        w1a_hi, w1b_hi = wa_hi[:, 0:HID], wa_hi[:, HID:2 * HID]
        w1a_lo, w1b_lo = wa_lo[:, 0:HID], wa_lo[:, HID:2 * HID]
        w2_lo, w2_hi = wb_hi[:, 0:CHUNK], wb_hi[:, CHUNK:2 * CHUNK]
        ffn_dram = [nc.dram_tensor("ffn_" + n, shape, F32, kind="Internal").ap()
                    for n, shape in (("w1a", (DA, HID)), ("w1b", (2 * DB, HID)), ("w2", (128, CHUNK)))]
        gT = [t[:, :, :] for t in (q_pair, k_pair)]
        g_hi, g_lo = ([t[:, p * PAIRS * S:(p + 1) * PAIRS * S].rearrange("p (m s) -> p m s", s=S) for p in range(2)]
                      for t in (val_hi, lows))
        obuf = [On[:, :, :, :].rearrange("p t h f -> p (t h f)")[:, p * TC * D:(p + 1) * TC * D]
                .rearrange("p (t d) -> p t d", t=TC) for p in range(2)]

        def load(name):
            return sem("ld_" + name)
        ld_tok, ld_emb, ld_w, ld_rel, ld_hot, ld_proj, ld_ffn = map(
            load, ("tok", "emb", "w", "rel", "hot", "proj", "ffn"))
        iota_done = sem("iota_done")
        iota_cast = sem("iota_cast")
        clamped = sem("clamped")
        onehot_ready = sem("onehot_ready")
        zeroed = sem("zeroed")
        eps_set = sem("eps_set")
        t0_ready = sem("t0_ready")
        emb_full = sem("emb_full")
        h_ready = sem("h_ready")
        stats_done = sem("stats_done")
        mv_done = sem("mv_done")
        std_done = sem("std_done")
        rstd_done = sem("rstd_done")
        hn_ready = sem("hn_ready")
        fn_ready = sem("fn_ready")
        raw_in = [sem(f"raw_in{n}") for n in range(4)]
        raw_hi = sem("raw_hi")
        raw_lo = sem("raw_lo")
        ffn_in_dram = sem("ffn_in_dram")
        ffn_raw = sem("ffn_raw")
        ffn_hi = sem("ffn_hi")
        ffn_split = sem("ffn_split")
        bias_added = sem("bias_added")
        filled = {kind: sem("filled_" + kind) for kind in TILES}
        moved = {kind: sem("moved_" + kind) for kind in TILES}
        moved_hi = {kind: sem("moved_hi_" + kind) for kind in ("x", "ow")}
        k_ready = sem("k_ready")
        v_ready = sem("v_ready")
        front_dma = sem("front_dma")
        k_sent = sem("k_sent")
        scores_ready = sem("scores_ready")
        negmax_ready = sem("negmax_ready")
        probs_ready = sem("probs_ready")
        pt_full = sem("pt_full")
        pt_ready = sem("pt_ready")
        pv_done = sem("pv_done")
        rden_done = sem("rden_done")
        u_done = sem("u_done")
        fx_full = sem("fx_full")
        fx_hi = sem("fx_hi")
        fx_lo = sem("fx_lo")
        f1_full = sem("f1_full")
        g_hi_ready = sem("g_hi_ready")
        g_lo_ready = sem("g_lo_ready")
        g_ready = sem("g_ready")
        f2_full = sem("f2_full")
        o_ready = [sem(f"o_ready{p}") for p in range(2)]
        o_sent = [sem(f"o_sent{p}") for p in range(2)]

        def in_order(b, steps, first, before):
            seq = list(before)
            out_steps = []
            for tl in steps:
                cur = []
                for kind, j in tl:
                    tb = b.after(1) if kind in FRONT else b.after(-1)
                    n = len(seq) - G_BANKS
                    cur.append((tb, kind, j, (first + n) % G_BANKS, seq[n]))
                    seq.append((tb, kind, j))
                out_steps.append(cur)
            return out_steps

        def last_tiles(b):
            return [(b, "v", j) for j in (0, 1, 2, 3)]

        def tiles(b):
            static = b.i is None
            steps = plan(b.exists(-1), b.exists(1))
            if static and b.k == 0:
                return in_order(b, steps, FRONT_TILES, last_tiles(b))
            return in_order(b, steps, 0, last_tiles(b))

        FRONT_TILES = sum(TILES[k] for k in FRONT)
        first_front = in_order(Batch(-1), plan(False, True), 0, [None] * G_BANKS)
        tail = [(Batch(B - 2), kind, j) for step in plan(True, False) for kind, j in step]
        last_tail = in_order(Batch(B), plan(True, False), 2 * FRONT_TILES + len(tail), tail[-G_BANKS:])

        whole, upper, lower = slice(0, 128), slice(0, 64), slice(64, 128)
        chunks = []
        for c in range(0, 3 * H * DH, CHUNK):
            cols = slice(c, c + CHUNK)
            chunks.append((qkw[0:DA, cols], [whole], wa_hi[:, cols], (wa_lo[:, cols], whole)))
            chunks.append((qkw[DA:D, cols], [upper, lower], wb_hi[:, cols], (wb_lo[:, cols], upper)))
        width = (NGRP + 1) * 128 // 4
        for c in range(0, 4 * width, width):
            cols = slice(c, c + width)
            chunks.append((val_rel[:, cols], [upper, lower], val_hi[:, cols], (val_lo[:, cols], lower)))

        block = ctx.enter_context(nc.Block())

        @block.sync
        def _(sp):
            sp.dma_start(tok_sb, tok.rearrange("b s -> (b s)").partition_broadcast(VOCAB)).then_inc(ld_tok, 16)
            sp.dma_start(etab_sb, etab).then_inc(ld_emb, 16)
            sp.dma_start(pe_sb, pe.rearrange("(t p) d -> p t d", p=128)).then_inc(ld_emb, 16)
            for n, (src, rows, _, _) in enumerate(chunks):
                if n >= 4:
                    sp.wait_ge(raw_lo, n - 3)
                for dst in rows:
                    sp.dma_start(raw[n % 4][dst, 0:src.shape[1]], src).then_inc(raw_in[n % 4], 16)
                if n == 3:
                    sp.wait_ge(zeroed, 1)
                    for e in range(2):
                        r = slice(64 * e, 64 * e + 64)
                        sp.dma_start(key_rel_sb[r, :, 32 * e:32 * e + 32], key_rel).then_inc(ld_rel, 16)
                        sp.dma_start(key_t0_sb[r, :], key_t0).then_inc(ld_rel, 16)
                    sp.dma_start(val_t0_sb[:], val_t0.rearrange("(o a) d -> o a d", o=1)).then_inc(ld_rel, 16)
            sp.wait_ge(raw_lo, len(chunks))
            for p in range(2):
                for t in range(TC):
                    sp.dma_start(V[p][:, t, :, DH:AUG],
                                 val_hot[128 * t:128 * t + 128, :].unsqueeze(1).to_broadcast([128, H, REL])).then_inc(ld_hot, 16)

            def known(value):
                return value if isinstance(value, int) else sp.snap(value)

            def place_front(b):
                qk_used = known(b.at(H, -H))
                ready = [known(b.at(n, n)) for n in (TILES["q"], 1, TILES["a"], TILES["b"])]
                wait(sp, scores_ready, qk_used)
                for src, dst, staged, n, sent in ((k_pair, K, k_ready, ready[1], k_sent),
                                                  (q_pair, Q, moved["q"], ready[0], front_dma)):
                    sp.wait_ge(staged, n)
                    for e in range(2):
                        sp.dma_start(dst[b.par][0:DH, e::2, :], src[64 * e:64 * e + 64, :, :]).then_inc(sent, 16)
                for src, kind, r0, n, ev in ((a_stage, "a", DH, ROWS, ready[2]), (b_stage, "b", DH + ROWS, SIDE, ready[3])):
                    sp.wait_ge(moved[kind], ev)
                    for e in range(2):
                        sp.dma_start(Q[b.par][r0:r0 + n, e::2, :], src[32 * e:32 * e + n, :, :]).then_inc(front_dma, 16)

            place_front(Batch(0))

            def batch(b):
                if b.exists(1):
                    place_front(b.after(1))

            for k in range(B):
                batch(Batch(k))
            sp.wait_ge(filled["v"], TILES["v"] * B)
            sp.wait_ge(ffn_in_dram, 16 * 4)
            for src, dst in zip(ffn_dram, (w1a_lo, w1b_lo, w2_lo)):
                sp.dma_start(dst.bitcast(F32), src).then_inc(ffn_raw, 16)
            with sp.Fori(0, B // 2) as i:
                for p in range(2):
                    sent, at = known(i + 1), known(Batch(p, i).at(1))
                    sp.wait_ge(o_ready[p], sent)
                    sp.dma_start(out[bass.ds(at, 1), :, :].rearrange("b (t p) d -> p (b t) d", p=128),
                                 obuf[p]).then_inc(o_sent[p], 16)
            for p in range(2):
                sp.wait_ge(o_sent[p], 16 * (B // 2))

        @block.gpsimd
        def _(pool):
            pool.iota(iota_i[:], [[0, 1]], base=0, channel_multiplier=1).then_inc(iota_done, 1)
            pool.memset(key_rel_sb[:], 0.0).then_inc(zeroed, 1)
            for n, (src, _, hi, (lo, rows)) in enumerate(chunks):
                pool.wait_ge(raw_hi, n + 1)
                if n > 0:
                    pool.wait_ge(raw_lo, n)
                high_low(pool, lo, raw[n % 4][rows, 0:src.shape[1]], hi[rows]).then_inc(raw_lo, 1)
            pool.wait_ge(raw_lo, len(chunks))
            pool.wait_ge(ld_proj, 32)
            for t in range(B):
                pool.wait_ge(hn_ready, t + 1)
                pool.tensor_tensor(h_sb[:, TC * t:TC * t + TC, :], h_sb[:, TC * t:TC * t + TC, :],
                                   pb_sb[:].unsqueeze(1).to_broadcast([128, TC, D]), ALU.add).then_inc(bias_added, 1)
            pool.wait_ge(ffn_raw, 48)
            for n, (hi, lo) in enumerate(((w1a_hi, w1a_lo), (w1b_hi, w1b_lo), (w2_hi, w2_lo))):
                pool.tensor_copy(hi, lo.bitcast(F32)).then_inc(ffn_hi, 1)
                pool.wait_ge(ffn_hi, n + 1)
                high_low(pool, lo, lo.bitcast(F32), hi).then_inc(ffn_split, 1)
            for b in range(B):
                pool.wait_ge(g_hi_ready, b + 1)
                if b >= 2:
                    pool.wait_ge(f2_full, b - 1)
                high_low(pool, g_lo[b % 2], gT[b % 2], g_hi[b % 2]).then_inc(g_lo_ready, 1)

        def split_x(eng, on_act, b, G, hi_sem, hi_count):
            p = b.par
            if on_act:
                eng.activation(x_hi[:], G[:, :].rearrange("p (a s) -> p a s", a=2), ACT.Copy).then_inc(hi_sem, 1)
            else:
                eng.wait_ge(hi_sem, hi_count)
                high_low(eng, x_hi[DB:128, 1, :], G[DB:128, S:2 * S], x_hi[DB:128, 1, :])

        def evacuate(eng, on_act, b, kind, j, bk):
            G = g_bank[bk]
            p = b.par
            eng.wait_ge(filled[kind], b.at(TILES[kind], j + 1))

            def copy(dst, src, scale=1.0):
                if on_act:
                    return eng.activation(dst, src, ACT.Copy, scale=scale)
                if scale != 1.0:
                    return eng.tensor_scalar(dst, src, scale, None, ALU.mult)
                return eng.tensor_copy(dst, src)

            if kind == "x" and on_act:
                wait(eng, filled["v"], b.at(4))
            if j == 0 and kind in ("q", "k"):
                wait(eng, front_dma, b.at(16 * FRONT_DMAS))
            if j == 0 and kind == "a":
                eng.wait_ge(k_sent, b.at(32, 32))
            if j == 0 and kind == "v":
                wait(eng, pv_done, b.at(H, -H))
            if j == 0 and kind == "ow" and on_act:
                if b.exists(1):
                    eng.wait_ge(filled["v"], b.at(4, 8))
                else:
                    eng.wait_ge(filled["o"], b.at(1))
            if kind == "ra" and j == 0:
                eng.wait_ge(moved["ow"], b.at(PAIRS, PAIRS))
            if kind == "rc" and j == 0:
                eng.wait_ge(moved["ra"], b.at(TILES["ra"], TILES["ra"]))

            if kind in ("q", "k"):
                dst = {"q": q_pair, "k": k_pair}[kind]
                ins = copy(dst[:, 2 * j:2 * j + 2, :], G[:, :].rearrange("p (r s) -> p r s", r=2),
                           SCALE if kind == "q" else 1.0)
            elif kind == "ow" and on_act:
                copy(OT[:, j, :], G[:, 0:S])
                copy(WT[:, j, :], G[:, S:2 * S]).then_inc(moved_hi["ow"], 1)
                return
            elif kind == "ow":
                eng.wait_ge(moved_hi["ow"], b.at(PAIRS, j + 1))
                ins = high_low(eng, WT[0:64, j, :], G[0:64, S:2 * S], WT[0:64, j, :])
            elif kind == "x":
                split_x(eng, on_act, b, G, moved_hi["x"], b.at(1, 1))
                if on_act:
                    return
                ins = high_low(eng, x_lo[:], G[:, 0:S], x_hi[:, 0, :])
            elif kind == "v":
                ins = copy(V[p][:, j // 2, 6 * (j % 2):6 * (j % 2) + 6, 0:DH],
                           G[:, 0:6 * DH].rearrange("p (h d) -> p h d", h=6))
            elif kind == "o":
                o = h_sb[:, bass.ds(b.at(TC), TC), :]
                ins = eng.tensor_tensor(o, G[:, 0:TC * D].rearrange("p (t d) -> p t d", t=TC), o, ALU.add)
            elif kind in ("a", "ra"):
                g = R_TILES[j]
                n = len(g)
                dst, src = (a_stage, G[0:64]) if kind == "a" else (OT[:], G[:])
                dst_g = dst[:, :, 1 + SIDE * g[0]:1 + SIDE * (g[0] + n)]
                src_g = src[:, 0:n * RN].rearrange("p (q r) -> p r q", r=PAIRS)
                ins = copy(dst_g, src_g) if kind == "a" else eng.tensor_tensor(dst_g, src_g, dst_g, ALU.add)
                if j == len(R_TILES) - 1:
                    c0 = n * RN
                    if kind == "a":
                        copy(a_stage[:, :, 0], G[0:64, c0:c0 + PAIRS])
                        ins = copy(b_stage[:, :, 0], G[0:64, c0 + PAIRS:c0 + 2 * PAIRS])
                    else:
                        ins = eng.tensor_tensor(OT[:, :, 0], G[:, c0:c0 + PAIRS], OT[:, :, 0], ALU.add)
            elif kind in ("b", "rc"):
                g = C_TILES[j]
                dst, src = (b_stage, G[0:64]) if kind == "b" else (OT[:], G[:])
                dst_g = dst[:, :, 1:S].rearrange("p r (a c) -> p r c a", c=SIDE)[:, :, g[0]:g[0] + CPT, :]
                src_g = src[:, 0:CPT * CN].rearrange("p (c a r) -> p r c a", c=CPT, r=PAIRS)
                ins = copy(dst_g, src_g) if kind == "b" else eng.tensor_tensor(dst_g, src_g, dst_g, ALU.add)
            ins.then_inc(moved[kind], 1)

        @block.scalar
        def _(act):
            act.dma_start(ident[:], ident_in).then_inc(ld_emb, 16)
            act.dma_start(pw_sb[:], proj_w.rearrange("(r p) n -> p r n", p=128)).then_inc(ld_proj, 16)
            act.dma_start(pb_sb[:], proj_b.partition_broadcast(128)).then_inc(ld_proj, 16)
            for p in range(2):
                act.dma_start(K[p][DH:AUG, :, :], key_hot.unsqueeze(1).to_broadcast([REL, H, S])).then_inc(ld_hot, 16)
            act.dma_start(b1_sb[:], b1_in).then_inc(ld_ffn, 16)
            for dst, src in ((ffn_dram[0], w1_in[0:DA, :]), (ffn_dram[1][0:DB, :], w1_in[DA:D, :]),
                             (ffn_dram[1][DB:128, :], w1_in[DA:D, :]),
                             (ffn_dram[2].rearrange("p (m n) -> p m n", n=D), w2_in.rearrange("(m p) n -> p m n", p=128))):
                act.dma_start(dst, src).then_inc(ffn_in_dram, 16)

            def split(n):
                src, _, hi, _ = chunks[n]
                act.wait_ge(raw_in[n % 4], 16 * sum(len(chunks[m][1]) for m in range(n % 4, n + 1, 4)))
                act.activation(hi, raw[n % 4][:, 0:src.shape[1]], ACT.Copy).then_inc(raw_hi, 1)

            for n in range(4):
                split(n)

            def std(r):
                act.wait_ge(mv_done, r)
                act.activation(rstd[:], mv[:, :, 1], ACT.Sqrt, bias=eps_sb[:, 0:1]).then_inc(std_done, 1)

            act.wait_ge(eps_set, 1)
            std(1)
            for n in range(4, len(chunks)):
                split(n)

            def exps(b, h):
                act.wait_ge(negmax_ready, b.at(H, h + 1))
                wait(act, pt_full, b.at(H, h - 1))
                for t in range(TC):
                    ins = act.activation(P[h % 2][:, t, :], score_bank[h % 2][:, t * S:t * S + S], ACT.Exp,
                                         bias=negmax[:, h % 4, t:t + 1],
                                         accum_out=den[:, h // 2, h % 2, t:t + 1])
                ins.then_inc(probs_ready, 1)

            def move_pt(b, h):
                act.wait_ge(pt_full, b.at(H, h + 1))
                wait(act, pv_done, b.at(H, h - 1))
                act.activation(PT[h % 2][:], pt_bank[:, :].rearrange("p (k q) -> p k q", k=TC),
                               ACT.Copy).then_inc(pt_ready, 1)

            def side(tl):
                for tb, kind, j, bk, _ in tl:
                    if kind in ON_ACT:
                        evacuate(act, True, tb, kind, j, bk)

            def batch(b):
                for s, tl in enumerate(tiles(b)):
                    exps(b, s)
                    if s >= 1:
                        move_pt(b, s - 1)
                    elif b.exists(-1):
                        move_pt(b.after(-1), H - 1)
                    side(tl)

            for tl in first_front:
                side(tl)
            batch(Batch(0))
            with act.Fori(0, (B - 2) // 2) as i:
                batch(Batch(1, i))
                batch(Batch(2, i))
            batch(Batch(B - 1))
            move_pt(Batch(B - 1), H - 1)
            for tl in last_tail:
                side(tl)

            std(2)
            act.wait_ge(ld_ffn, 16)

            def block_ff(b):
                act.wait_ge(fx_full, b.at(1, 1))
                wait(act, f1_full, b.at(3))
                split_x(act, True, b, bank[6], fx_hi, None)
                wait(act, g_lo_ready, b.at(1, -1))
                for m in range(HID // 128):
                    if m % 2 == 0:
                        act.wait_ge(f1_full, b.at(3, m // 2 + 1))
                    act.activation(gT[b.par][:, m, :], bank[3 * b.par + m // 2][:, (m % 2) * S:(m % 2) * S + S],
                                   ACT.Gelu, bias=b1_sb[:, m:m + 1]).then_inc(g_ready, 1)

            for p in range(2):
                block_ff(Batch(p))
            with act.Fori(0, B // 2 - 1) as i:
                for p in range(2):
                    block_ff(Batch(2 + p, i))

        @block.vector
        def _(dve):
            dve.memset(eps_sb[:], EPS).then_inc(eps_set, 1)
            dve.wait_ge(iota_done, 1)
            dve.tensor_copy(iota_f[:], iota_i[:]).then_inc(iota_cast, 1)
            dve.wait_ge(iota_cast, 1)
            dve.wait_ge(ld_tok, 16)
            for c in range(B):
                dve.tensor_scalar(onehot[:, c * S:c * S + S], tok_sb[:, c * S:c * S + S], float(VOCAB - 1),
                                  iota_f[0:VOCAB, 0:1], ALU.min, ALU.is_equal).then_inc(onehot_ready, 1)
            dve.wait_ge(ld_emb, 48)
            for c in range(B):
                dve.wait_ge(emb_full, c + 1)
                dve.scalar_tensor_tensor(out=h_sb[:, TC * c:TC * c + TC, :].rearrange("p t d -> p (t d)"),
                                         in0=bank[c][:, 0:TC * D], scalar=math.sqrt(D),
                                         in1=pe_sb.rearrange("p t d -> p (t d)"),
                                         op0=ALU.mult, op1=ALU.add).then_inc(h_ready, 1)

            def moments(b):
                for t in range(TC):
                    ins = dve.bn_stats(stats[:, bass.ds(b.at(TC, t), 1), :].rearrange("p a d -> p (a d)"),
                                       h_sb[:, bass.ds(b.at(TC, t), 1), :].rearrange("p a d -> p (a d)"))
                ins.then_inc(stats_done, 1)

            def inverse_std(r):
                dve.wait_ge(stats_done, r * B)
                for t in range(B * TC):
                    ins = dve.bn_aggr(mv[:, t, :], stats[:, t, :])
                ins.then_inc(mv_done, 1)
                dve.wait_ge(std_done, r)
                dve.reciprocal(rstd[:], rstd[:]).then_inc(rstd_done, 1)
                dve.wait_ge(rstd_done, r)

            def normalise(b, turned, done):
                wait(dve, turned, b.at(1))
                for t in range(TC):
                    n = bass.ds(b.at(TC, t), 1)
                    ins = dve.tensor_scalar(hn[:, t, :], h_sb[:, n, :].rearrange("p a d -> p (a d)"),
                                            mv[:, n, 0], rstd[:, n], ALU.subtract, ALU.mult)
                ins.then_inc(done, 1)

            for c in range(B):
                dve.wait_ge(h_ready, c + 1)
                moments(Batch(c))
            inverse_std(1)
            dve.wait_ge(ld_rel, 16 * 5)
            dve.tensor_tensor(key_t0s[:], key_t0_sb[:, 0:1], key_t0_sb[:, 1:2], ALU.add).then_inc(t0_ready, 1)
            dve.tensor_tensor(val_t0s[:], val_t0_sb[:, 0, :], val_t0_sb[:, 1, :], ALU.add).then_inc(t0_ready, 1)
            dve.wait_ge(t0_ready, 2)

            def maxima(b, h):
                dve.wait_ge(scores_ready, b.at(H, h + 1))
                dve.tensor_reduce(negmax[:, h % 4, :], score_bank[h % 2][:, :].rearrange("p (t s) -> p t s", t=TC),
                                  AX.X, ALU.max, negate=True).then_inc(negmax_ready, 1)

            def normalise_u(b, pr):
                wait(dve, filled["ow"], b.at(PAIRS, pr + 1 - PAIRS))
                dve.wait_ge(probs_ready, b.at(H, 2 * pr + 2))
                dve.reciprocal(rden[:, pr, :, :], den[:, pr, :, :]).then_inc(rden_done, 1)
                dve.wait_ge(rden_done, b.at(PAIRS, pr + 1))
                dve.wait_ge(pv_done, b.at(H, 2 * pr + 2))
                U = u_bank[:, 0:2 * TC * AUG].rearrange("p (e t f) -> p e t f", e=2, t=TC)
                dve.tensor_tensor(On[:, :, 2 * pr:2 * pr + 2, :].rearrange("p t e f -> p e t f"), U[:, :, :, 0:DH],
                                  rden[:, pr, :, :].unsqueeze(3).to_broadcast([128, 2, TC, DH]), ALU.mult)
                for t in range(TC):
                    ins = dve.tensor_tensor(Wn[:, t, pr, :, :, :].rearrange("p c e f -> p e c f"),
                                            U[:, :, t, DH:AUG].unsqueeze(2).to_broadcast([128, 2, 2, REL]),
                                            rden[:, pr, :, t].unsqueeze(2).unsqueeze(3).to_broadcast([128, 2, 2, REL]),
                                            ALU.mult)
                ins.then_inc(u_done, 1)

            def side(tl):
                for tb, kind, j, bk, _ in tl:
                    if kind == "x":
                        normalise(tb, filled["x"], hn_ready)
                    if kind == "o":
                        dve.wait_ge(bias_added, tb.at(1, 1))
                    if kind in ON_DVE:
                        evacuate(dve, False, tb, kind, j, bk)
                    if kind == "o":
                        dve.wait_ge(moved["o"], tb.at(1, 1))
                        moments(tb)
                    if kind == "k" and j == PAIRS // 2 - 1:
                        dve.wait_ge(moved["k"], tb.at(TILES["k"], TILES["k"]))
                        dve.tensor_scalar(k_pair[:, :, 0], k_pair[:, :, 0], key_t0s[:, 0:1], None,
                                          ALU.add).then_inc(k_ready, 1)
                    if kind == "v" and j == 3:
                        dve.wait_ge(moved["v"], tb.at(4, 4))
                        v0 = V[tb.par][0:1, 0, :, 0:DH]
                        dve.tensor_tensor(v0, v0, val_t0s[0:1, :].unsqueeze(1).to_broadcast([1, H, DH]),
                                          ALU.add).then_inc(v_ready, 1)

            def batch(b):
                for s, tl in enumerate(tiles(b)):
                    maxima(b, s)
                    if s >= 3 and s % 2 == 1:
                        normalise_u(b, (s - 3) // 2)
                    elif s == 1 and b.exists(-1):
                        normalise_u(b.after(-1), PAIRS - 1)
                    side(tl)

            for tl in first_front:
                side(tl)
            batch(Batch(0))
            with dve.Fori(0, (B - 2) // 2) as i:
                batch(Batch(1, i))
                batch(Batch(2, i))
            batch(Batch(B - 1))
            normalise_u(Batch(B - 1), PAIRS - 1)
            for tl in last_tail:
                side(tl)

            inverse_std(2)

            def results(b):
                p = b.par
                dve.wait_ge(f2_full, b.at(1, 1))
                wait(dve, o_sent[p], b.half(16))
                dve.tensor_tensor(obuf[p], bank[7][:, 0:TC * D].rearrange("p (t d) -> p t d", t=TC),
                                  h_sb[:, bass.ds(b.at(TC), TC), :], ALU.add).then_inc(o_ready[p], 1)

            def norm_block(b):
                normalise(b, fx_full, fn_ready)

            def low_x(b):
                split_x(dve, False, b, bank[6], fx_hi, b.at(1, 1))
                high_low(dve, x_lo[:], bank[6][:, 0:S], x_hi[:, 0, :]).then_inc(fx_lo, 1)

            def high_g(b):
                dve.wait_ge(g_ready, b.at(6, 6))
                wait(dve, f2_full, b.at(1, -1))
                dve.tensor_copy(g_hi[b.par], gT[b.par]).then_inc(g_hi_ready, 1)

            def block_ff(b):
                if b.exists(2):
                    norm_block(b.after(2))
                if b.exists(1):
                    high_g(b.after(1))
                if b.exists(2):
                    low_x(b.after(2))
                results(b)

            for p in range(2):
                norm_block(Batch(p))
                low_x(Batch(p))
            high_g(Batch(0))
            for p in range(2):
                block_ff(Batch(p))
            with dve.Fori(0, B // 2 - 2) as i:
                for p in range(2):
                    block_ff(Batch(2 + p, i))
            for k in (B - 2, B - 1):
                block_ff(Batch(k))

        @block.tensor
        def _(pe_):
            mm = pe_.matmul
            pe_.wait_ge(ld_emb, 48)
            for c in range(B):
                pe_.wait_ge(onehot_ready, c + 1)
                for t in range(TC):
                    n = TC * c + t
                    ins = mm(bank[c][:, t * D:t * D + D], onehot[:, n * 128:n * 128 + 128], etab_sb,
                             start=True, stop=True)
                ins.then_inc(emb_full, 1)

            def turn_x(G):
                for t in range(TC):
                    pe_.transpose(G[:, t * 128:t * 128 + 128], hn[:, t, 0:DA], ident[:])
                for t in range(TC):
                    for f0 in (D - 128, DA):
                        ins = pe_.transpose(G[0:D - f0, S + t * 128:S + t * 128 + 128], hn[:, t, f0:D], ident[:])
                return ins

            def project(out_t, x_stays, xs, w, ws):
                wah, wal, wbh, wbl = (part[:, ws] for part in w)
                terms = ((x_hi[:, 0, xs], wah), (x_lo[:, xs], wah), (x_hi[:, 0, xs], wal),
                         (x_hi[:, 1, xs], wbh), (x_hi[0:DB, 1, xs], wbl[0:DB]))
                for n, (x, wt) in enumerate(terms):
                    ins = mm(out_t, *((x, wt) if x_stays else (wt, x)), start=(n == 0), stop=(n == len(terms) - 1))
                return ins

            w_qkv = (wa_hi, wa_lo, wb_hi, wb_lo)
            w_in = (w1a_hi, w1a_lo, w1b_hi, w1b_lo)
            pe_.wait_ge(raw_lo, len(chunks))
            pe_.wait_ge(ld_rel, 16 * 5)
            pe_.wait_ge(ld_hot, 16 * 2 * (1 + TC))
            pe_.wait_ge(ld_proj, 32)

            def scores(b, h):
                if h == 0:
                    pe_.wait_ge(k_sent, b.at(32, 32))
                    pe_.wait_ge(front_dma, b.at(16 * FRONT_DMAS, 16 * FRONT_DMAS))
                wait(pe_, probs_ready, b.at(H, h - 1))
                for t in range(TC):
                    ins = mm(score_bank[h % 2][:, t * S:t * S + S], Q[b.par][:, h, t * 128:t * 128 + 128],
                             K[b.par][:, h, :], start=True, stop=True)
                ins.then_inc(scores_ready, 1)

            def turn_p(b, h):
                pe_.wait_ge(probs_ready, b.at(H, h + 1))
                wait(pe_, pt_ready, b.at(H, h))
                for k in range(TC):
                    for t in range(TC):
                        ins = pe_.transpose(pt_bank[:, k * S + t * 128:k * S + t * 128 + 128],
                                            P[h % 2][:, t, k * 128:k * 128 + 128], ident[:])
                ins.then_inc(pt_full, 1)

            def values(b, h):
                if h == 0:
                    pe_.wait_ge(v_ready, b.at(1, 1))
                if h % 2 == 0:
                    wait(pe_, u_done, b.at(PAIRS, h // 2))
                pe_.wait_ge(pt_ready, b.at(H, h + 1))
                for t in range(TC):
                    for k in range(TC):
                        c0 = (TC * (h % 2) + t) * AUG
                        ins = mm(u_bank[:, c0:c0 + AUG], PT[h % 2][:, k, t * 128:t * 128 + 128],
                                 V[b.par][:, k, h, :], start=(k == 0), stop=(k == TC - 1))
                ins.then_inc(pv_done, 1)

            def by_query(t):
                return t[:, :, :].rearrange("p r s -> p s r")

            def rel_values(out_t, g, queries):
                cols = slice(g * 128, g * 128 + 128)
                mm(out_t, val_hi[:, cols], by_query(WT)[:, queries, :], start=True, stop=False)
                return mm(out_t, val_lo[:, cols], by_query(WT[64:128])[:, queries, :], start=False, stop=True)

            def fill(b, kind, j, bk, before):
                G = g_bank[bk]
                if before is not None:
                    b0, kind0, j0 = before
                    wait(pe_, moved[kind0], b0.at(TILES[kind0], j0 + 1))
                p = b.par
                if kind == "x":
                    pe_.wait_ge(hn_ready, b.at(1, 1))
                    ins = turn_x(G)
                elif kind in "qk":
                    if kind == "k" and j == 0:
                        pe_.wait_ge(moved["x"], b.at(1, 1))
                    for r in range(2):
                        n0 = (0 if kind == "q" else H * DH) + (2 * j + r) * 128
                        ins = project(G[:, r * S:r * S + S], False, slice(0, S), w_qkv, slice(n0, n0 + 128))
                elif kind == "v":
                    n0 = 2 * H * DH + (j % 2) * 6 * DH
                    t0 = (j // 2) * 128
                    ins = project(G[:, 0:6 * DH], True, slice(t0, t0 + 128), w_qkv, slice(n0, n0 + 6 * DH))
                elif kind == "a":
                    if j == 0:
                        pe_.wait_ge(moved["q"], b.at(3, 3))
                    for m, g in enumerate(R_TILES[j]):
                        ins = mm(G[0:64, m * RN:m * RN + RN], key_rel_sb[:, g, :],
                                 by_query(q_pair)[:, 1 + SIDE * g:1 + SIDE * g + SIDE, :], start=True, stop=True)
                    if j == len(R_TILES) - 1:
                        for m in range(2):
                            c0 = len(R_TILES[j]) * RN + m * PAIRS
                            ins = mm(G[0:64, c0:c0 + PAIRS], key_rel_sb[:, NGRP + m, :], q_pair[:, :, 0],
                                     start=True, stop=True)
                elif kind == "b":
                    for m, g in enumerate(C_TILES[j]):
                        ins = mm(G[0:64, m * CN:m * CN + CN], key_rel_sb[:, ROWS + g, :],
                                 by_query(q_pair)[:, 1 + g:S:SIDE, :], start=True, stop=True)
                elif kind == "ow":
                    if j == 0:
                        pe_.wait_ge(u_done, b.at(PAIRS, PAIRS))
                    for t in range(TC):
                        pe_.transpose(G[:, t * 128:t * 128 + 128],
                                      On[:, t, 2 * j:2 * j + 2, :].rearrange("p e f -> p (e f)"), ident[:])
                    for t in range(TC):
                        ins = pe_.transpose(G[:, S + t * 128:S + t * 128 + 128],
                                            Wn[:, t, j, :, :, :].rearrange("p c e f -> p (c e f)"), ident[:])
                elif kind == "ra":
                    if j == 0:
                        pe_.wait_ge(moved["ow"], b.at(PAIRS, PAIRS))
                    for m, g in enumerate(R_TILES[j]):
                        ins = rel_values(G[:, m * RN:m * RN + RN], g, slice(1 + SIDE * g, 1 + SIDE * g + SIDE))
                    if j == len(R_TILES) - 1:
                        c0 = len(R_TILES[j]) * RN
                        ins = rel_values(G[:, c0:c0 + PAIRS], NGRP, slice(0, 1))
                elif kind == "rc":
                    for m, g in enumerate(C_TILES[j]):
                        ins = rel_values(G[:, m * CN:m * CN + CN], ROWS + g, slice(1 + g, S, SIDE))
                elif kind == "o":
                    if j == 0:
                        pe_.wait_ge(moved["rc"], b.at(3, 3))
                    for t in range(TC):
                        for r in range(PAIRS):
                            ins = mm(G[:, t * D:t * D + D], OT[:, r, t * 128:t * 128 + 128], pw_sb[:, r, :],
                                     start=(r == 0), stop=(r == PAIRS - 1))
                ins.then_inc(filled[kind], 1)

            def side(tl):
                for tile in tl:
                    fill(*tile)

            def batch(b):
                for s, tl in enumerate(tiles(b)):
                    scores(b, s)
                    if s >= 1:
                        turn_p(b, s - 1)
                    elif b.exists(-1):
                        turn_p(b.after(-1), H - 1)
                    if s >= 2:
                        values(b, s - 2)
                    elif b.exists(-1):
                        values(b.after(-1), H - 2 + s)
                    side(tl)

            for tl in first_front:
                side(tl)
            batch(Batch(0))
            with pe_.Fori(0, (B - 2) // 2) as i:
                batch(Batch(1, i))
                batch(Batch(2, i))
            batch(Batch(B - 1))
            turn_p(Batch(B - 1), H - 1)
            for h in (H - 2, H - 1):
                values(Batch(B - 1), h)
            for tl in last_tail:
                side(tl)

            pe_.wait_ge(ffn_split, 3)

            def turn_block(b):
                pe_.wait_ge(fn_ready, b.at(1, 1))
                wait(pe_, fx_lo, b.at(1))
                turn_x(bank[6]).then_inc(fx_full, 1)

            def hidden(b):
                pe_.wait_ge(fx_lo, b.at(1, 1))
                wait(pe_, g_ready, b.at(6, -6))
                for m in range(HID // 128):
                    ins = project(bank[3 * b.par + m // 2][:, (m % 2) * S:(m % 2) * S + S], False,
                                  slice(0, S), w_in, slice(m * 128, m * 128 + 128))
                    if m % 2 == 1:
                        ins.then_inc(f1_full, 1)

            def outputs(b):
                pe_.wait_ge(g_lo_ready, b.at(1, 1))
                wait(pe_, o_ready[1 - b.par], b.half(1, b.par))
                for t in range(TC):
                    q = slice(t * 128, t * 128 + 128)
                    for m in range(HID // 128):
                        w = slice(m * D, m * D + D)
                        terms = ((g_hi, w2_hi), (g_lo, w2_hi), (g_hi, w2_lo))
                        for n, (g, wt) in enumerate(terms):
                            ins = mm(bank[7][:, t * D:t * D + D], g[b.par][:, m, q], wt[:, w],
                                     start=(m == 0 and n == 0), stop=(m == HID // 128 - 1 and n == 2))
                ins.then_inc(f2_full, 1)

            def block_ff(b):
                if b.exists(2):
                    turn_block(b.after(2))
                outputs(b)
                if b.exists(2):
                    hidden(b.after(2))

            for p in range(2):
                turn_block(Batch(p))
                hidden(Batch(p))
            for p in range(2):
                block_ff(Batch(p))
            with pe_.Fori(0, B // 2 - 2) as i:
                for p in range(2):
                    block_ff(Batch(2 + p, i))
            for k in (B - 2, B - 1):
                block_ff(Batch(k))


def rel_windows(table, n):
    q, k = np.arange(n)[:, None], np.arange(n)[None, :]
    return table[np.clip(k - q, -MAX_REL, MAX_REL) + MAX_REL + 1]


def kernel(**inputs):
    import concourse.bacc as bacc
    from concourse.bass_utils import run_bass_kernel_spmd

    a = {k.split("_", 2)[-1] if k.startswith("L0_") else k: np.asarray(v) for k, v in inputs.items()}
    code = np.arange(VOCAB - a["special_W"].shape[0])
    etab = np.concatenate([
        np.concatenate([a["color_W"][code // 16], a["shape_W"][code % 16 // 4], a["quantity_W"][code % 4]], axis=-1),
        a["special_W"]])
    even = np.arange(0, D, 2, dtype=np.float32)
    angle = np.arange(S, dtype=np.float32)[:, None] * np.exp(-(even / np.float32(D)) * np.float32(math.log(10000.0)))
    pe = np.stack([np.sin(angle), np.cos(angle)], axis=-1).reshape(S, D).astype(np.float32)

    key_rel = np.zeros((NGRP + 2, REL, DH), np.float32)
    key_rel[:ROWS, :ROWS] = rel_windows(a["tab_kv"], ROWS)
    key_rel[ROWS:NGRP, :SIDE] = rel_windows(a["tab_kh"], SIDE)
    key_rel[NGRP, :ROWS] = a["tab_kv"][0]
    key_rel[NGRP + 1, :SIDE] = a["tab_kh"][0]
    val_rel = np.zeros((NGRP + 1, REL, DH), np.float32)
    val_rel[:ROWS, :ROWS] = rel_windows(a["tab_vv"], ROWS)
    val_rel[ROWS:NGRP, ROWS:] = rel_windows(a["tab_vh"], SIDE)
    val_rel[NGRP, :ROWS] = a["tab_vv"][0]
    val_rel[NGRP, ROWS:] = a["tab_vh"][0]
    val_pairs = np.zeros((NGRP + 1, 2 * REL, 2 * DH), np.float32)
    val_pairs[:, :REL, :DH] = val_rel
    val_pairs[:, REL:, DH:] = val_rel
    token = np.arange(1, S)
    hot = np.zeros((S, REL), np.float32)
    hot[token, (token - 1) // SIDE] = 1.0
    hot[token, ROWS + (token - 1) % SIDE] = 1.0

    arrays = {
        "tok": a["x"],
        "etab": etab,
        "pe": pe,
        "qkw": a["qkv_w"].T,
        "proj_w": a["proj_w"].T,
        "proj_b": a["proj_b"],
        "key_rel": key_rel.transpose(2, 0, 1),
        "key_t0": np.stack([a["tab_kv"][0], a["tab_kh"][0]], axis=1),
        "val_rel": val_pairs.transpose(1, 0, 2).reshape(2 * REL, -1),
        "val_t0": np.stack([a["tab_vv"][0], a["tab_vh"][0]]),
        "key_hot": hot.T,
        "val_hot": hot,
        "ident": np.eye(128, dtype=np.float32),
        "w1": a["in_weight"].T,
        "b1": a["in_bias"].reshape(HID // 128, 128).T,
        "w2": a["out_weight"],
    }
    nc = bacc.Bacc("TRN2", target_bir_lowering=False, num_devices=1)
    arrays = {k: np.ascontiguousarray(v) for k, v in arrays.items()}
    args = [nc.dram_tensor("in_" + k, v.shape, mybir.dt.from_np(v.dtype), kind="ExternalInput").ap()
            for k, v in arrays.items()]
    args.append(nc.dram_tensor("out", (B, S, D), F32, kind="ExternalOutput").ap())
    build(nc, *args)
    r = run_bass_kernel_spmd(nc, [{"in_" + k: v for k, v in arrays.items()}], core_ids=[0])
    return r.results[0]["out"]
```

```python
from contextlib import ExitStack
import math

import numpy as np
import concourse.bass as bass
from concourse import mybir

F32 = mybir.dt.float32
F32R = mybir.dt.float32r
I32 = mybir.dt.int32
ALU = mybir.AluOpType
ACT = mybir.ActivationFunctionType
AX = mybir.AxisListType

B, S, D = 8, 256, 192
H, DH = 12, 64
HALF = H // 2
PAIRS = H // 2
HID = 768
DA, DB = 128, D - 128
TC = S // 128
SIDE = int((S - 1) ** 0.5)
ROWS = (S - 1) // SIDE
MAX_REL = 14
REL = ROWS + SIDE
AUG = DH + REL
NGRP = ROWS + SIDE
VOCAB = 70
EPS = 1e-5
SCALE = DH ** -0.5
RPT, CPT = 5, 5
R_TILES = [range(g, min(g + RPT, ROWS)) for g in range(0, ROWS, RPT)]
C_TILES = [range(g, g + CPT) for g in range(0, SIDE, CPT)]
RN, CN = PAIRS * SIDE, PAIRS * ROWS
NTOK = S * B
CHUNK = H * DH


def plan(with_tail, with_front):
    steps = [[] for _ in range(H)]
    def put(s, *tiles):
        steps[s] += tiles
    tail = lambda s, *tiles: put(s, *tiles) if with_tail else None
    front = lambda s, *tiles: put(s, *tiles) if with_front else None
    front(0, ("x", 0))
    tail(0, ("c0", 0))
    front(1, ("k", 0), ("k", 1))
    tail(1, ("c0", 1))
    front(2, ("k", 2), ("q", 0))
    tail(2, ("c0", 2))
    front(3, ("q", 1), ("q", 2))
    tail(3, ("r1", 0))
    front(4, ("a", 0), ("a", 1))
    tail(4, ("r1", 1), ("r1", 2))
    front(5, ("a", 2), ("a", 3))
    tail(5, ("r1", 3), ("c1", 0))
    front(6, ("b", 0), ("b", 1))
    tail(6, ("c1", 1))
    tail(7, ("c1", 2))
    front(7, ("b", 2))
    tail(8, ("o", 0))
    front(8, ("v", 0), ("v", 1))
    tail(9, ("o", 1))
    put(9, ("r0", 0))
    put(10, ("r0", 1), ("r0", 2))
    front(10, ("v", 2), ("v", 3))
    put(11, ("r0", 3))
    return steps


TILES = {"x": 1, "q": 3, "k": 3, "a": len(R_TILES), "b": len(C_TILES), "v": 4,
         "r0": len(R_TILES), "c0": len(C_TILES), "r1": len(R_TILES), "c1": len(C_TILES), "o": TC}
FRONT = ("x", "q", "k", "a", "b", "v")
TAIL = ("c0", "r1", "c1", "o")
FRONT_TILES = sum(TILES[k] for k in FRONT)
OWN_TILES = TILES["r0"]
MERGED = sum(TILES.values())
FRONT_DMAS = 6
G_BANKS = 4
ON_ACT = {"x", "q", "k", "a", "b", "v"}
ON_DVE = {"x", "v", "r0", "c0", "r1", "c1", "o"}


class Batch:
    def __init__(self, k, i=None):
        self.k, self.i = k, i
        self.par = k % 2

    def at(self, n, c=0):
        if self.i is None:
            return n * self.k + c
        return self.i * (2 * n) + (n * self.k + c)

    def half(self, n, c=0):
        if self.i is None:
            return n * (self.k // 2) + c
        return self.i * n + (n * (self.k // 2) + c)

    def after(self, d):
        return Batch(self.k + d, self.i)

    def exists(self, d):
        return self.i is not None or 0 <= self.k + d < B


TURN, WEIGH = 2, 3


def behind(b, s, lag, do):
    if lag <= s < H + lag:
        do(b, s - lag)
    elif s < lag and b.exists(-1):
        do(b.after(-1), H + s - lag)


def wait(eng, sem, value):
    if not isinstance(value, int) or value > 0:
        eng.wait_ge(sem, value)


def high_low(eng, low, whole, high):
    return eng.tensor_tensor(low, whole, high.bitcast(F32), ALU.subtract)


def build(nc, tok, etab, pe, qkw, proj_w, proj_b, key_rel, key_t0, val_rel, val_t0, key_hot, val_hot,
          ident_in, w1_in, b1_in, w2_in, out):
    with ExitStack() as ctx:
        def sb(name, shape, dt=F32):
            return ctx.enter_context(nc.sbuf_tensor(name, shape, dt))

        def sem(name):
            return ctx.enter_context(nc.semaphore(name))

        bank = [ctx.enter_context(nc.psum_tensor(f"bank{n}", [128, 512], F32)) for n in range(8)]
        score_bank, pt_bank, u_bank, g_bank = bank[0:2], bank[2], bank[3], bank[4:8]

        ident = sb("ident", [128, 128])
        iota_i = sb("iota_i", [128, 1], I32)
        iota_f = sb("iota_f", [128, 1])
        eps_sb = sb("eps_sb", [128, 1])
        unused = sb("unused", [128, 1])
        wa_hi = sb("wa_hi", [DA, 3 * H * DH], F32R)
        wa_lo = sb("wa_lo", [DA, 3 * H * DH], F32R)
        wb_hi = sb("wb_hi", [2 * DB, 3 * H * DH], F32R)
        wb_lo = sb("wb_lo", [2 * DB, 3 * H * DH], F32R)[DB:2 * DB]
        val_sb = sb("val_sb", [3 * REL, (NGRP + 1) * DH], F32R)
        pw_sb = sb("pw_sb", [128, PAIRS, D])
        pb_sb = sb("pb_sb", [128, D])
        key_rel_sb = sb("key_rel_sb", [128, NGRP + 2, 64])
        key_t0_sb = sb("key_t0_sb", [128, 2])
        key_t0s = sb("key_t0s", [128, 1])
        val_t0_sb = sb("val_t0_sb", [1, 2, DH])
        val_t0s = sb("val_t0s", [1, DH])
        b1_sb = sb("b1_sb", [128, HID // 128])
        h_sb = sb("h_sb", [128, B * TC, D])
        stats = sb("stats", [128, B * TC, 6])
        mv = sb("mv", [128, B * TC, 2])
        rstd = sb("rstd", [128, B * TC])
        hn = sb("hn", [128, TC, D])
        x_hi = sb("x_hi", [128, 2, S], F32R)
        x_lo = sb("x_lo", [DA, S], F32R)
        q_pair = sb("q_pair", [128, PAIRS, S])
        k_pair = sb("k_pair", [128, PAIRS, S])
        a_stage, b_stage = k_pair[0:64], k_pair[64:128]
        Q = [sb(f"Q{p}", [AUG, H, S]) for p in range(2)]
        K = [sb(f"K{p}", [128, H, S]) for p in range(2)]
        V_hi = [sb(f"V_hi{p}", [128, TC, H, AUG], F32R) for p in range(2)]
        V_lo = [sb(f"V_lo{p}", [128, TC, H, DH], F32R) for p in range(2)]
        tok_sb = Q[0][0:VOCAB].rearrange("p h s -> p (h s)")[:, 0:NTOK].bitcast(I32)
        onehot = Q[1][0:VOCAB].rearrange("p h s -> p (h s)")[:, 0:NTOK]
        negmax = sb("negmax", [128, 4, TC])
        den = sb("den", [128, 4, TC])
        rden = sb("rden", [128, 4, TC])
        P = [sb(f"P{p}", [128, TC, S]) for p in range(3)]
        PT_hi = [sb(f"PT_hi{p}", [128, TC, S], F32R) for p in range(2)]
        PT_lo = [sb(f"PT_lo{p}", [128, TC, S], F32R) for p in range(2)]
        OT = [sb(f"OT{p}", [128, PAIRS, S]) for p in range(2)]
        WT = [sb(f"WT{f}", [3 * REL, HALF, S], F32R) for f in range(2)]
        etab_sb = OT[0][0:VOCAB].rearrange("p r s -> p (r s)")[:, 0:D]
        pe_sb = P[0][:].rearrange("p t s -> p (t s)")[:, 0:TC * D].rearrange("p (t d) -> p t d", t=TC)
        hot_sb = P[1][:].rearrange("p t s -> p (t s)")[:, 0:TC * REL].rearrange("p (t f) -> p t f", t=TC)
        raw = [t[:].rearrange("p h s -> p (h s)")[:, c:c + CHUNK]
               for t, chunks_in in ((K[1], 4), (OT[1], 2)) for c in range(0, chunks_in * CHUNK, CHUNK)]
        val_raw = K[1][0:3 * REL].rearrange("p h s -> p (h s)")[:, 0:(NGRP + 1) * DH]
        w1a_hi, w1b_hi = wa_hi[:, 0:HID], wa_hi[:, HID:2 * HID]
        w1a_lo, w1b_lo = wa_lo[:, 0:HID], wa_lo[:, HID:2 * HID]
        w2_sb = K[B % 2][:].rearrange("p h s -> p (h s)")[:, 0:HID // 128 * D].rearrange("p (m n) -> p m n", n=D)
        w1a_dram, w1b_dram = (nc.dram_tensor(n, shape, F32, kind="Internal").ap() for n, shape in
                              (("w1a_raw", (DA, HID)), ("w1b_raw", (2 * DB, HID))))
        gT = [t[:, :, :] for t in (q_pair, k_pair)]
        obuf = [OT[p][:, :, :].rearrange("p r s -> p (r s)")[:, 0:TC * D].rearrange("p (t d) -> p t d", t=TC)
                for p in range(2)]

        def load(name):
            return sem("ld_" + name)
        ld_tok, ld_emb, ld_rel, ld_hot, ld_hot_v, ld_proj, ld_b1 = map(
            load, ("tok", "emb", "rel", "hot", "hot_v", "proj", "b1"))
        iota_done = sem("iota_done")
        iota_cast = sem("iota_cast")
        onehot_ready = sem("onehot_ready")
        zeroed = sem("zeroed")
        eps_set = sem("eps_set")
        t0_ready = sem("t0_ready")
        emb_full = sem("emb_full")
        h_ready = sem("h_ready")
        stats_done = sem("stats_done")
        mv_done = sem("mv_done")
        std_done = sem("std_done")
        rstd_done = sem("rstd_done")
        hn_ready = sem("hn_ready")
        fn_ready = sem("fn_ready")
        raw_in = [sem(f"raw_in{n}") for n in range(len(raw))]
        raw_hi = sem("raw_hi")
        raw_lo = sem("raw_lo")
        in_dram = sem("in_dram")
        ld_val = sem("ld_val")
        ld_w2 = sem("ld_w2")
        hot_placed = sem("hot_placed")
        ffn_raw = sem("ffn_raw")
        ffn_hi = sem("ffn_hi")
        ffn_split = sem("ffn_split")
        bias_added = sem("bias_added")
        filled = {kind: sem("filled_" + kind) for kind in TILES}
        moved = {kind: sem("moved_" + kind) for kind in TILES}
        moved_hi = {kind: sem("moved_hi_" + kind) for kind in ("x", "v")}
        k_ready = sem("k_ready")
        v0_added = sem("v0_added")
        front_dma = sem("front_dma")
        k_sent = sem("k_sent")
        scores_ready = sem("scores_ready")
        negmax_ready = sem("negmax_ready")
        probs_ready = sem("probs_ready")
        pt_full = sem("pt_full")
        rden_ready = sem("rden_ready")
        probs_scaled = sem("probs_scaled")
        pt_hi_ready = sem("pt_hi_ready")
        pt_lo_ready = sem("pt_lo_ready")
        pv_done = sem("pv_done")
        ot_ready = sem("ot_ready")
        wt_hi_ready = sem("wt_hi_ready")
        wt_ready = sem("wt_ready")
        val_split = sem("val_split")
        fx_full = sem("fx_full")
        fx_hi = sem("fx_hi")
        fx_lo = sem("fx_lo")
        f1_full = sem("f1_full")
        g_ready = sem("g_ready")
        f2_full = sem("f2_full")
        o_ready = [sem(f"o_ready{p}") for p in range(2)]
        o_sent = [sem(f"o_sent{p}") for p in range(2)]

        def in_order(b, steps, first, before):
            seq = list(before)
            out_steps = []
            for tl in steps:
                cur = []
                for kind, j in tl:
                    tb = b.after(1) if kind in FRONT else b.after(-1) if kind in TAIL else b
                    n = len(seq) - G_BANKS
                    cur.append((tb, kind, j, (first + n) % G_BANKS, seq[n]))
                    seq.append((tb, kind, j))
                out_steps.append(cur)
            return out_steps

        def tiles(b):
            if b.i is None and b.k == 0:
                first, before = FRONT_TILES, [(b, "v", j) for j in range(4)]
            else:
                first = 2 * FRONT_TILES + OWN_TILES + (b.k - 1) * MERGED
                before = [(b.after(-1), "r0", 2), (b, "v", 2), (b, "v", 3), (b.after(-1), "r0", 3)]
            return in_order(b, plan(b.exists(-1), b.exists(1)), first, before)

        first_front = [[tile for tile in tl if tile[1] in FRONT]
                       for tl in in_order(Batch(-1), [[t for t in tl if t[0] in FRONT] for tl in plan(False, True)],
                                          0, [None] * G_BANKS)]
        EMB_BANKS = 8 - G_BANKS
        first_embeddings = range(EMB_BANKS)
        embeddings_behind = {0: (4, 5), 2: (6, 7)}
        beside_last = [(Batch(B - 1 if kind == "r0" else B - 2), kind, j)
                       for step in plan(True, False) for kind, j in step]
        last_tail = in_order(Batch(B), [[t for t in tl if t[0] in TAIL] for tl in plan(True, False)],
                             2 * FRONT_TILES + OWN_TILES + (B - 2) * MERGED + len(beside_last),
                             beside_last[-G_BANKS:])
        last_c0, last_rel, last_out = last_tail[:3], last_tail[3:8], last_tail[8:]

        def x_bank(b):
            return bank[7] if b.i is None and b.k == 0 else bank[3]

        def f1_bank(b, m):
            return bank[(0, 4)[b.par] + m // 2]

        whole, upper, lower = slice(0, 128), slice(0, 64), slice(64, 128)
        chunks = []
        for part in (1, 0, 2):
            cols = slice(part * CHUNK, part * CHUNK + CHUNK)
            chunks.append((qkw[0:DA, cols], [whole], wa_hi[:, cols], wa_lo[:, cols], whole))
            chunks.append((qkw[DA:D, cols], [upper, lower], wb_hi[:, cols], wb_lo[:, cols], lower))

        passes = [slice(0, TC), slice(TC, B * TC), slice(0, (B - 1) * TC), slice((B - 1) * TC, B * TC)]

        block = ctx.enter_context(nc.Block())

        @block.sync
        def _(sp):
            sp.dma_start(tok_sb, tok.rearrange("b s -> (b s)").partition_broadcast(VOCAB)).then_inc(ld_tok, 16)
            sp.dma_start(etab_sb, etab).then_inc(ld_emb, 16)
            sp.dma_start(pe_sb, pe.rearrange("(t p) d -> p t d", p=128)).then_inc(ld_emb, 16)
            for n, (src, rows, *_) in enumerate(chunks):
                for dst in rows:
                    sp.dma_start(raw[n][dst], src).then_inc(raw_in[n], 16)
            sp.wait_ge(zeroed, 1)
            for e in range(2):
                r = slice(64 * e, 64 * e + 64)
                sp.dma_start(key_rel_sb[r, :, 32 * e:32 * e + 32], key_rel).then_inc(ld_rel, 16)
                sp.dma_start(key_t0_sb[r, :], key_t0).then_inc(ld_rel, 16)
            sp.dma_start(val_t0_sb[:], val_t0.rearrange("(o a) d -> o a d", o=1)).then_inc(ld_rel, 16)
            sp.dma_start(hot_sb, val_hot.rearrange("(t p) f -> p t f", p=128)).then_inc(ld_hot_v, 16)
            sp.dma_start(K[0][DH:AUG, :, :], key_hot.unsqueeze(1).to_broadcast([REL, H, S])).then_inc(ld_hot, 16)
            sp.dma_start(pb_sb[:], proj_b.partition_broadcast(128)).then_inc(ld_proj, 16)
            sp.dma_start(pw_sb[:], proj_w.rearrange("(r p) n -> p r n", p=128)).then_inc(ld_proj, 16)
            sp.dma_start(b1_sb[:], b1_in).then_inc(ld_b1, 16)
            for dst, src in ((w1a_dram, w1_in[0:DA, :]),
                             (w1b_dram[0:DB, :], w1_in[DA:D, :]), (w1b_dram[DB:128, :], w1_in[DA:D, :])):
                sp.dma_start(dst, src).then_inc(in_dram, 16)
            sp.wait_ge(raw_lo, 4)
            for n in range(3):
                sp.dma_start(val_raw[REL * n:REL * n + REL], val_rel).then_inc(ld_val, 16)

            def known(value):
                return value if isinstance(value, int) else sp.snap(value)

            def place_front(b):
                qk_used = known(b.at(H, -H))
                ready = [known(b.at(n, n)) for n in (TILES["q"], 1, TILES["a"], TILES["b"])]
                wait(sp, scores_ready, qk_used)
                for src, dst, staged, n, sent in ((k_pair, K, k_ready, ready[1], k_sent),
                                                  (q_pair, Q, moved["q"], ready[0], front_dma)):
                    sp.wait_ge(staged, n)
                    for e in range(2):
                        sp.dma_start(dst[b.par][0:DH, e::2, :], src[64 * e:64 * e + 64, :, :]).then_inc(sent, 16)
                for src, kind, r0, n, ev in ((a_stage, "a", DH, ROWS, ready[2]), (b_stage, "b", DH + ROWS, SIDE, ready[3])):
                    sp.wait_ge(moved[kind], ev)
                    for e in range(2):
                        sp.dma_start(Q[b.par][r0:r0 + n, e::2, :], src[32 * e:32 * e + n, :, :]).then_inc(front_dma, 16)

            place_front(Batch(0))
            sp.wait_ge(val_split, 2)
            sp.dma_start(K[1][DH:AUG, :, :], key_hot.unsqueeze(1).to_broadcast([REL, H, S])).then_inc(ld_hot, 16)

            for k in range(1, B):
                place_front(Batch(k))
            sp.wait_ge(scores_ready, H * (B - 1))
            sp.dma_start(w2_sb, w2_in.rearrange("(m p) n -> p m n", p=128)).then_inc(ld_w2, 16)
            sp.wait_ge(filled["v"], TILES["v"] * B)
            sp.wait_ge(in_dram, 48)
            for src, dst in ((w1a_dram, w1a_lo), (w1b_dram, w1b_lo)):
                sp.dma_start(dst.bitcast(F32), src).then_inc(ffn_raw, 16)
            with sp.Fori(0, B // 2) as i:
                for p in range(2):
                    sent, at = known(i + 1), known(Batch(p, i).at(1))
                    sp.wait_ge(o_ready[p], sent)
                    sp.dma_start(out[bass.ds(at, 1), :, :].rearrange("b (t p) d -> p (b t) d", p=128),
                                 obuf[p]).then_inc(o_sent[p], 16)
            for p in range(2):
                sp.wait_ge(o_sent[p], 16 * (B // 2))

        @block.gpsimd
        def _(pool):
            pool.iota(iota_i[:], [[0, 1]], base=0, channel_multiplier=1).then_inc(iota_done, 1)
            pool.memset(key_rel_sb[:], 0.0).then_inc(zeroed, 1)
            for n, (_, _, hi, lo, rows) in enumerate(chunks):
                pool.wait_ge(raw_hi, n + 1)
                if n > 0:
                    pool.wait_ge(raw_lo, n)
                high_low(pool, lo, raw[n][rows], hi[rows]).then_inc(raw_lo, 1)
            pool.wait_ge(raw_lo, len(chunks))
            pool.wait_ge(ld_hot_v, 16)
            for p in range(2):
                for t in range(TC):
                    pool.tensor_copy(V_hi[p][:, t, :, DH:AUG],
                                     hot_sb[:, t, :].unsqueeze(1).to_broadcast([128, H, REL])).then_inc(hot_placed, 1)

            pool.wait_ge(hot_placed, 2 * TC)
            pool.wait_ge(val_split, 1)
            high_low(pool, val_sb[2 * REL:3 * REL], val_raw[2 * REL:3 * REL],
                     val_sb[2 * REL:3 * REL]).then_inc(val_split, 1)
            pool.wait_ge(val_split, 2)

            def add_bias(b):
                pool.wait_ge(hn_ready, b.at(1, 1))
                o = h_sb[:, bass.ds(b.at(TC), TC), :]
                pool.tensor_tensor(o, o, pb_sb[:].unsqueeze(1).to_broadcast([128, TC, D]),
                                   ALU.add).then_inc(bias_added, 1)

            def scale(b, h):
                pool.wait_ge(rden_ready, b.at(H, h + 1))
                pool.tensor_tensor(P[h % 3][:], P[h % 3][:], rden[:, h % 4, :].unsqueeze(2).to_broadcast([128, TC, S]),
                                   ALU.mult).then_inc(probs_scaled, 1)

            def batch(b):
                for h in range(H):
                    scale(b, h)
                    if h == 1 and b.exists(1):
                        add_bias(b.after(1))

            def split_w1(n):
                hi, lo = ((w1a_hi, w1a_lo), (w1b_hi, w1b_lo))[n // 4]
                cols = slice(n // 2 % 2 * (HID // 2), n // 2 % 2 * (HID // 2) + HID // 2)
                if n % 2 == 0:
                    pool.tensor_copy(hi[:, cols], lo[:, cols].bitcast(F32)).then_inc(ffn_hi, 1)
                else:
                    pool.wait_ge(ffn_hi, n // 2 + 1)
                    high_low(pool, lo[:, cols], lo[:, cols].bitcast(F32), hi[:, cols]).then_inc(ffn_split, 1)

            pool.wait_ge(ld_proj, 32)
            add_bias(Batch(0))
            batch(Batch(0))
            with pool.Fori(0, (B - 2) // 2) as i:
                batch(Batch(1, i))
                batch(Batch(2, i))
            for h in range(H):
                scale(Batch(B - 1), h)
                if h == 3:
                    pool.wait_ge(ffn_raw, 32)
                if 3 <= h < 11:
                    split_w1(h - 3)

        def split_x(eng, on_act, b, G, hi_sem, hi_count):
            p = b.par
            if on_act:
                eng.activation(x_hi[:, 0, :], G[:, 0:S], ACT.Copy)
                eng.activation(x_hi[DB:128, 1, :], G[0:DB, S:2 * S], ACT.Copy).then_inc(hi_sem, 1)
            else:
                eng.wait_ge(hi_sem, hi_count)
                high_low(eng, x_hi[0:DB, 1, :], G[0:DB, S:2 * S], x_hi[DB:128, 1, :])

        def evacuate(eng, on_act, b, kind, j, bk):
            G = g_bank[bk]
            p = b.par
            eng.wait_ge(filled[kind], b.at(TILES[kind], j + 1))

            def copy(dst, src, scale=1.0):
                if on_act:
                    return eng.activation(dst, src, ACT.Copy, scale=scale)
                if scale != 1.0:
                    return eng.tensor_scalar(dst, src, scale, None, ALU.mult)
                return eng.tensor_copy(dst, src)

            if kind == "x" and on_act:
                wait(eng, filled["v"], b.at(4))
            if j == 0 and kind in ("q", "k"):
                wait(eng, front_dma, b.at(16 * FRONT_DMAS))
            if j == 0 and kind == "a":
                eng.wait_ge(k_sent, b.at(32, 32))
            if j == 0 and kind == "v" and on_act:
                wait(eng, pv_done, b.at(H, -H))
            if kind in ("r0", "r1") and j == 0:
                eng.wait_ge(ot_ready, b.at(H, HALF if kind == "r0" else H))
            if kind in ("c0", "c1") and j == 0:
                rows = "r" + kind[1]
                eng.wait_ge(moved[rows], b.at(TILES[rows], TILES[rows]))

            if kind in ("q", "k"):
                dst = {"q": q_pair, "k": k_pair}[kind]
                ins = copy(dst[:, 2 * j:2 * j + 2, :], G[:, :].rearrange("p (r s) -> p r s", r=2),
                           SCALE if kind == "q" else 1.0)
            elif kind == "x":
                split_x(eng, on_act, b, G, moved_hi["x"], b.at(1, 1))
                if on_act:
                    return
                ins = high_low(eng, x_lo[:], G[:, 0:S], x_hi[:, 0, :])
            elif kind == "v":
                t, heads = j // 2, slice(6 * (j % 2), 6 * (j % 2) + 6)
                hi, whole_v = V_hi[p][:, t, heads, 0:DH], G[:, 0:6 * DH].rearrange("p (h d) -> p h d", h=6)
                if on_act:
                    if t == 0:
                        eng.wait_ge(v0_added, b.at(2, j + 1))
                    copy(hi, whole_v).then_inc(moved_hi["v"], 1)
                    return
                if t == 0:
                    v0 = whole_v[0:1]
                    eng.tensor_tensor(v0, v0, val_t0s[0:1, :].unsqueeze(1).to_broadcast([1, 6, DH]),
                                      ALU.add).then_inc(v0_added, 1)
                eng.wait_ge(moved_hi["v"], b.at(TILES["v"], j + 1))
                ins = high_low(eng, V_lo[p][:, t, heads, :], whole_v, hi)
            elif kind == "o":
                o = h_sb[:, bass.ds(b.at(TC, j), 1), :].rearrange("p t d -> p (t d)")
                ins = eng.tensor_tensor(o, G[:, 0:D], o, ALU.add)
            elif kind == "a":
                g = R_TILES[j]
                n = len(g)
                ins = copy(a_stage[:, :, 1 + SIDE * g[0]:1 + SIDE * (g[0] + n)],
                           G[0:64, 0:n * RN].rearrange("p (q r) -> p r q", r=PAIRS))
                if j == len(R_TILES) - 1:
                    c0 = n * RN
                    copy(a_stage[:, :, 0], G[0:64, c0:c0 + PAIRS])
                    ins = copy(b_stage[:, :, 0], G[0:64, c0 + PAIRS:c0 + 2 * PAIRS])
            elif kind == "b":
                g = C_TILES[j]
                ins = copy(b_stage[:, :, 1:S].rearrange("p r (a c) -> p r c a", c=SIDE)[:, :, g[0]:g[0] + CPT, :],
                           G[0:64, 0:CPT * CN].rearrange("p (c a r) -> p r c a", c=CPT, r=PAIRS))
            else:
                pair = slice(int(kind[1]) * HALF // 2, (int(kind[1]) + 1) * HALF // 2)
                for e in range(2):
                    o = OT[p][DH * e:DH * e + DH, pair, :]
                    if kind[0] == "r":
                        g = R_TILES[j]
                        n = len(g)
                        dst = o[:, :, 1 + SIDE * g[0]:1 + SIDE * (g[0] + n)]
                        src = G[0:DH, 0:n * RN].rearrange("p (q r e) -> p e r q", r=HALF // 2, e=2)[:, e]
                    else:
                        g = C_TILES[j]
                        dst = o[:, :, 1:S].rearrange("p r (a c) -> p r c a", c=SIDE)[:, :, g[0]:g[0] + CPT, :]
                        src = G[0:DH, 0:CPT * CN].rearrange("p (c a r e) -> p e r c a", c=CPT, r=HALF // 2, e=2)[:, e]
                    ins = eng.tensor_tensor(dst, src, dst, ALU.add)
                    if kind[0] == "r" and j == len(R_TILES) - 1:
                        c0 = n * RN
                        ins = eng.tensor_tensor(o[:, :, 0], G[0:DH, c0:c0 + HALF].rearrange("p (r e) -> p e r", e=2)[:, e],
                                                o[:, :, 0], ALU.add)
            ins.then_inc(moved[kind], 1)

        @block.scalar
        def _(act):
            act.dma_start(ident[:], ident_in).then_inc(ld_emb, 16)

            def split(n):
                act.wait_ge(raw_in[n], 16 * len(chunks[n][1]))
                act.activation(chunks[n][2], raw[n], ACT.Copy).then_inc(raw_hi, 1)

            def std(r):
                act.wait_ge(mv_done, r + 1)
                act.activation(rstd[:, passes[r]], mv[:, passes[r], 1], ACT.Sqrt, bias=eps_sb[:, 0:1]).then_inc(std_done, 1)

            split(0)
            split(1)
            act.wait_ge(eps_set, 1)
            std(0)
            split(2)

            def exps(b, h):
                act.wait_ge(negmax_ready, b.at(H, h + 1))
                wait(act, pt_full, b.at(H, h - 2))
                for t in range(TC):
                    ins = act.activation(P[h % 3][:, t, :], score_bank[h % 2][:, t * S:t * S + S], ACT.Exp,
                                         bias=negmax[:, h % 4, t:t + 1],
                                         accum_out=den[:, h % 4, t:t + 1])
                ins.then_inc(probs_ready, 1)

            def move_pt(b, h):
                act.wait_ge(pt_full, b.at(H, h + 1))
                wait(act, pv_done, b.at(H, h - 1))
                act.activation(PT_hi[h % 2][:], pt_bank[:, :].rearrange("p (k q) -> p k q", k=TC),
                               ACT.Copy).then_inc(pt_hi_ready, 1)

            def move_ot(b, h):
                act.wait_ge(pv_done, b.at(H, h + 1))
                for r0 in (0, 2 * REL):
                    ins = act.activation(WT[h // HALF][r0:r0 + REL, h % HALF, :], u_bank[DH:AUG, 0:S], ACT.Copy)
                ins.then_inc(wt_hi_ready, 1)
                act.activation(OT[b.par][DH * (h % 2):DH * (h % 2) + DH, h // 2, :],
                               u_bank[0:DH, 0:S], ACT.Copy).then_inc(ot_ready, 1)

            def side(tl):
                for tb, kind, j, bk, _ in tl:
                    if kind in ON_ACT:
                        evacuate(act, True, tb, kind, j, bk)

            def batch(b):
                for s, tl in enumerate(tiles(b)):
                    behind(b, s, TURN, move_pt)
                    behind(b, s, WEIGH, move_ot)
                    exps(b, s)
                    side(tl)

            for step, tl in enumerate(first_front):
                side(tl)
                if step == 0:
                    for n in range(3, len(chunks)):
                        split(n)
                if step == 3:
                    std(1)
                    act.wait_ge(ld_val, 48)
                    act.activation(val_sb[:], val_raw, ACT.Copy).then_inc(val_split, 1)
                    act.activation(unused[:], eps_sb[:], ACT.Exp)
            act.wait_ge(hot_placed, 2 * TC)
            batch(Batch(0))
            with act.Fori(0, (B - 2) // 2) as i:
                batch(Batch(1, i))
                batch(Batch(2, i))
            batch(Batch(B - 1))
            last = Batch(B - 1)
            behind(last, H, TURN, move_pt)
            behind(last, H, WEIGH, move_ot)
            std(2)
            behind(last, H + 1, TURN, move_pt)
            behind(last, H + 1, WEIGH, move_ot)

            def high_x(b):
                act.wait_ge(fx_full, b.at(1, 1))
                wait(act, f1_full, b.at(3))
                split_x(act, True, b, x_bank(b), fx_hi, None)

            def gelu(b):
                wait(act, f2_full, b.at(1, -1))
                for m in range(HID // 128):
                    if m % 2 == 0:
                        act.wait_ge(f1_full, b.at(3, m // 2 + 1))
                    act.activation(gT[b.par][:, m, :], f1_bank(b, m)[:, (m % 2) * S:(m % 2) * S + S],
                                   ACT.Gelu, bias=b1_sb[:, m:m + 1]).then_inc(g_ready, 1)

            def block_ff(b):
                high_x(b)
                gelu(b)

            high_x(Batch(0))
            behind(last, H + 2, WEIGH, move_ot)
            act.activation(unused[:], eps_sb[:], ACT.Gelu)
            act.wait_ge(ld_b1, 16)
            gelu(Batch(0))
            high_x(Batch(1))
            std(3)
            gelu(Batch(1))
            with act.Fori(0, B // 2 - 1) as i:
                for p in range(2):
                    block_ff(Batch(2 + p, i))

        @block.vector
        def _(dve):
            dve.memset(eps_sb[:], EPS).then_inc(eps_set, 1)
            dve.wait_ge(iota_done, 1)
            dve.tensor_copy(iota_f[:], iota_i[:]).then_inc(iota_cast, 1)
            dve.wait_ge(iota_cast, 1)
            dve.wait_ge(ld_tok, 16)
            for c in range(B):
                dve.tensor_scalar(onehot[:, c * S:c * S + S], tok_sb[:, c * S:c * S + S], float(VOCAB - 1),
                                  iota_f[0:VOCAB, 0:1], ALU.min, ALU.is_equal).then_inc(onehot_ready, 1)

            def moments(b):
                for t in range(TC):
                    ins = dve.bn_stats(stats[:, bass.ds(b.at(TC, t), 1), :].rearrange("p a d -> p (a d)"),
                                       h_sb[:, bass.ds(b.at(TC, t), 1), :].rearrange("p a d -> p (a d)"))
                ins.then_inc(stats_done, 1)

            def aggregate(r):
                dve.wait_ge(stats_done, (1, B, 2 * B - 1, 2 * B)[r])
                for t in range(passes[r].start, passes[r].stop):
                    ins = dve.bn_aggr(mv[:, t, :], stats[:, t, :])
                ins.then_inc(mv_done, 1)

            def invert_std(r):
                dve.wait_ge(std_done, r + 1)
                dve.reciprocal(rstd[:, passes[r]], rstd[:, passes[r]]).then_inc(rstd_done, 1)
                dve.wait_ge(rstd_done, r + 1)

            def normalise(b, turned, done):
                wait(dve, turned, b.at(1))
                for t in range(TC):
                    n = bass.ds(b.at(TC, t), 1)
                    ins = dve.tensor_scalar(hn[:, t, :], h_sb[:, n, :].rearrange("p a d -> p (a d)"),
                                            mv[:, n, 0], rstd[:, n], ALU.subtract, ALU.mult)
                ins.then_inc(done, 1)

            dve.wait_ge(ld_emb, 48)

            def embed(c):
                dve.wait_ge(emb_full, c + 1)
                dve.scalar_tensor_tensor(out=h_sb[:, TC * c:TC * c + TC, :].rearrange("p t d -> p (t d)"),
                                         in0=bank[c % EMB_BANKS][:, 0:TC * D], scalar=math.sqrt(D),
                                         in1=pe_sb.rearrange("p t d -> p (t d)"),
                                         op0=ALU.mult, op1=ALU.add).then_inc(h_ready, 1)
                dve.wait_ge(h_ready, c + 1)
                moments(Batch(c))

            for c in first_embeddings:
                embed(c)
                if c == 0:
                    aggregate(0)
                if c == 2:
                    invert_std(0)
                    normalise(Batch(0), filled["x"], hn_ready)

            def maxima(b, h):
                dve.wait_ge(scores_ready, b.at(H, h + 1))
                dve.tensor_reduce(negmax[:, h % 4, :], score_bank[h % 2][:, :].rearrange("p (t s) -> p t s", t=TC),
                                  AX.X, ALU.max, negate=True).then_inc(negmax_ready, 1)

            def invert_sums(b, h):
                dve.wait_ge(probs_ready, b.at(H, h + 1))
                dve.reciprocal(rden[:, h % 4, :], den[:, h % 4, :]).then_inc(rden_ready, 1)

            def low_pt(b, h):
                dve.wait_ge(pt_hi_ready, b.at(H, h + 1))
                high_low(dve, PT_lo[h % 2][:], pt_bank[:, :].rearrange("p (k q) -> p k q", k=TC),
                         PT_hi[h % 2][:]).then_inc(pt_lo_ready, 1)

            def move_wt(b, h):
                dve.wait_ge(wt_hi_ready, b.at(H, h + 1))
                w = WT[h // HALF]
                high_low(dve, w[REL:2 * REL, h % HALF, :], u_bank[DH:AUG, 0:S],
                         w[2 * REL:3 * REL, h % HALF, :]).then_inc(wt_ready, 1)

            def side(tl):
                for tb, kind, j, bk, _ in tl:
                    if kind == "o" and j == 0:
                        dve.wait_ge(bias_added, tb.at(1, 1))
                    if kind in ON_DVE:
                        evacuate(dve, False, tb, kind, j, bk)
                    if kind == "o" and j == TC - 1:
                        dve.wait_ge(moved["o"], tb.at(TC, TC))
                        moments(tb)
                    if kind == "k" and j == PAIRS // 2 - 1:
                        dve.wait_ge(moved["k"], tb.at(TILES["k"], TILES["k"]))
                        dve.tensor_scalar(k_pair[:, :, 0], k_pair[:, :, 0], key_t0s[:, 0:1], None,
                                          ALU.add).then_inc(k_ready, 1)

            def batch(b):
                for s, tl in enumerate(tiles(b)):
                    if s == 0 and b.exists(1) and b.exists(-1):
                        normalise(b.after(1), filled["x"], hn_ready)
                    maxima(b, s)
                    behind(b, s, 1, invert_sums)
                    behind(b, s, TURN, low_pt)
                    behind(b, s, WEIGH, move_wt)
                    side(tl)

            for step, tl in enumerate(first_front):
                if step == 1:
                    dve.wait_ge(ld_rel, 16 * 5)
                    dve.tensor_tensor(key_t0s[:], key_t0_sb[:, 0:1], key_t0_sb[:, 1:2], ALU.add).then_inc(t0_ready, 1)
                    dve.tensor_tensor(val_t0s[:], val_t0_sb[:, 0, :], val_t0_sb[:, 1, :], ALU.add).then_inc(t0_ready, 1)
                    dve.wait_ge(t0_ready, 2)
                side(tl)
                for c in embeddings_behind.get(step, ()):
                    embed(c)
                if step == 2:
                    aggregate(1)
                if step == 6:
                    invert_std(1)
                    normalise(Batch(1), filled["x"], hn_ready)
            batch(Batch(0))
            with dve.Fori(0, (B - 2) // 2) as i:
                batch(Batch(1, i))
                batch(Batch(2, i))
            batch(Batch(B - 1))
            last = Batch(B - 1)
            aggregate(2)
            behind(last, H, 1, invert_sums)
            behind(last, H, TURN, low_pt)
            behind(last, H, WEIGH, move_wt)

            def results(b):
                p = b.par
                dve.wait_ge(f2_full, b.at(1, 1))
                wait(dve, o_sent[p], b.half(16))
                dve.tensor_tensor(obuf[p], bank[7][:, 0:TC * D].rearrange("p (t d) -> p t d", t=TC),
                                  h_sb[:, bass.ds(b.at(TC), TC), :], ALU.add).then_inc(o_ready[p], 1)

            def norm_block(b):
                normalise(b, fx_full, fn_ready)

            def low_x(b):
                split_x(dve, False, b, x_bank(b), fx_hi, b.at(1, 1))
                high_low(dve, x_lo[:], x_bank(b)[:, 0:S], x_hi[:, 0, :]).then_inc(fx_lo, 1)

            def block_ff(b):
                if b.exists(2):
                    norm_block(b.after(2))
                    low_x(b.after(2))
                results(b)

            invert_std(2)
            norm_block(Batch(0))
            behind(last, H + 1, TURN, low_pt)
            behind(last, H + 1, WEIGH, move_wt)
            low_x(Batch(0))
            behind(last, H + 2, WEIGH, move_wt)
            for tl in last_c0:
                side(tl)
            norm_block(Batch(1))
            for tl in last_rel:
                side(tl)
            low_x(Batch(1))
            for tl in last_out:
                side(tl)
            aggregate(3)
            invert_std(3)
            for p in range(2):
                block_ff(Batch(p))
            with dve.Fori(0, B // 2 - 2) as i:
                for p in range(2):
                    block_ff(Batch(2 + p, i))
            for k in (B - 2, B - 1):
                block_ff(Batch(k))

        @block.tensor
        def _(pe_):
            mm = pe_.matmul
            pe_.wait_ge(ld_emb, 48)

            def embed(c):
                pe_.wait_ge(onehot_ready, c + 1)
                if c >= EMB_BANKS:
                    pe_.wait_ge(h_ready, c - EMB_BANKS + 1)
                for t in range(TC):
                    n = TC * c + t
                    ins = mm(bank[c % EMB_BANKS][:, t * D:t * D + D], onehot[:, n * 128:n * 128 + 128], etab_sb,
                             start=True, stop=True)
                ins.then_inc(emb_full, 1)

            for c in first_embeddings:
                embed(c)

            def turn_x(G):
                for t in range(TC):
                    pe_.transpose(G[:, t * 128:t * 128 + 128], hn[:, t, 0:DA], ident[:])
                for t in range(TC):
                    ins = pe_.transpose(G[0:DB, S + t * 128:S + t * 128 + 128], hn[:, t, DA:D], ident[:])
                return ins

            def project(out_t, x_stays, xs, w, ws):
                wah, wal, wbh, wbl = (part[:, ws] for part in w)
                terms = ((x_hi[:, 0, xs], wah), (x_lo[:, xs], wah), (x_hi[:, 0, xs], wal),
                         (x_hi[:, 1, xs], wbh), (x_hi[DB:128, 1, xs], wbl))
                for n, (x, wt) in enumerate(terms):
                    ins = mm(out_t, *((x, wt) if x_stays else (wt, x)), start=(n == 0), stop=(n == len(terms) - 1))
                return ins

            w_qkv = (wa_hi, wa_lo, wb_hi, wb_lo)
            w_in = (w1a_hi, w1a_lo, w1b_hi, w1b_lo[DB:128])

            def scores(b, h):
                if h == 0:
                    pe_.wait_ge(k_sent, b.at(32, 32))
                    pe_.wait_ge(front_dma, b.at(16 * FRONT_DMAS, 16 * FRONT_DMAS))
                wait(pe_, probs_ready, b.at(H, h - 1))
                for t in range(TC):
                    ins = mm(score_bank[h % 2][:, t * S:t * S + S], Q[b.par][:, h, t * 128:t * 128 + 128],
                             K[b.par][0:AUG, h, :], start=True, stop=True)
                ins.then_inc(scores_ready, 1)

            def turn_p(b, h):
                pe_.wait_ge(probs_scaled, b.at(H, h + 1))
                wait(pe_, pt_lo_ready, b.at(H, h))
                for k in range(TC):
                    for t in range(TC):
                        ins = pe_.transpose(pt_bank[:, k * S + t * 128:k * S + t * 128 + 128],
                                            P[h % 3][:, t, k * 128:k * 128 + 128], ident[:])
                ins.then_inc(pt_full, 1)

            def values(b, h):
                if h == 0:
                    pe_.wait_ge(moved["v"], b.at(TILES["v"], TILES["v"]))
                wait(pe_, ot_ready, b.at(H, h))
                wait(pe_, wt_ready, b.at(H, h))
                pe_.wait_ge(pt_lo_ready, b.at(H, h + 1))
                p, U = b.par, u_bank[:, 0:S]
                for k in range(TC):
                    mm(U[0:AUG], V_hi[p][:, k, h, :], PT_hi[h % 2][:, k, :], start=(k == 0), stop=False)
                    mm(U[0:DH], V_lo[p][:, k, h, :], PT_hi[h % 2][:, k, :], start=False, stop=False)
                    ins = mm(U[0:AUG], V_hi[p][:, k, h, :], PT_lo[h % 2][:, k, :], start=False, stop=(k == TC - 1))
                ins.then_inc(pv_done, 1)

            def by_query(t):
                return t[:, :, :].rearrange("p r s -> p s r")

            def rel_values(out_t, f, g, queries):
                return mm(out_t, val_sb[:, g * DH:g * DH + DH], by_query(WT[f])[:, queries, :],
                          start=True, stop=True)

            def static_first(b):
                return b.i is None and b.k == 0

            def fill(b, kind, j, bk, before):
                G = g_bank[bk]
                if before is not None:
                    b0, kind0, j0 = before
                    wait(pe_, moved[kind0], b0.at(TILES[kind0], j0 + 1))
                p = b.par
                if kind == "x":
                    pe_.wait_ge(hn_ready, b.at(1, 1))
                    ins = turn_x(G)
                elif kind in "qk":
                    if kind == "k" and j == 0:
                        pe_.wait_ge(moved["x"], b.at(1, 1))
                    if static_first(b) and j == 0:
                        pe_.wait_ge(raw_lo, 2 if kind == "k" else 4)
                    for r in range(2):
                        n0 = (0 if kind == "q" else H * DH) + (2 * j + r) * 128
                        ins = project(G[:, r * S:r * S + S], False, slice(0, S), w_qkv, slice(n0, n0 + 128))
                elif kind == "v":
                    if static_first(b) and j == 0:
                        pe_.wait_ge(raw_lo, 6)
                    n0 = 2 * H * DH + (j % 2) * 6 * DH
                    t0 = (j // 2) * 128
                    ins = project(G[:, 0:6 * DH], True, slice(t0, t0 + 128), w_qkv, slice(n0, n0 + 6 * DH))
                elif kind == "a":
                    if static_first(b) and j == 0:
                        pe_.wait_ge(ld_rel, 16 * 5)
                    if j == 0:
                        pe_.wait_ge(moved["q"], b.at(3, 3))
                    for m, g in enumerate(R_TILES[j]):
                        ins = mm(G[0:64, m * RN:m * RN + RN], key_rel_sb[:, g, :],
                                 by_query(q_pair)[:, 1 + SIDE * g:1 + SIDE * g + SIDE, :], start=True, stop=True)
                    if j == len(R_TILES) - 1:
                        for m in range(2):
                            c0 = len(R_TILES[j]) * RN + m * PAIRS
                            ins = mm(G[0:64, c0:c0 + PAIRS], key_rel_sb[:, NGRP + m, :], q_pair[:, :, 0],
                                     start=True, stop=True)
                elif kind == "b":
                    for m, g in enumerate(C_TILES[j]):
                        ins = mm(G[0:64, m * CN:m * CN + CN], key_rel_sb[:, ROWS + g, :],
                                 by_query(q_pair)[:, 1 + g:S:SIDE, :], start=True, stop=True)
                elif kind[0] == "r":
                    f = int(kind[1])
                    if j == 0:
                        pe_.wait_ge(wt_ready, b.at(H, HALF * (f + 1)))
                    for m, g in enumerate(R_TILES[j]):
                        ins = rel_values(G[0:DH, m * RN:m * RN + RN], f, g, slice(1 + SIDE * g, 1 + SIDE * g + SIDE))
                    if j == len(R_TILES) - 1:
                        c0 = len(R_TILES[j]) * RN
                        ins = rel_values(G[0:DH, c0:c0 + HALF], f, NGRP, slice(0, 1))
                elif kind[0] == "c":
                    for m, g in enumerate(C_TILES[j]):
                        ins = rel_values(G[0:DH, m * CN:m * CN + CN], int(kind[1]), ROWS + g, slice(1 + g, S, SIDE))
                elif kind == "o":
                    if j == 0:
                        pe_.wait_ge(moved["c1"], b.at(TILES["c1"], TILES["c1"]))
                    for r in range(PAIRS):
                        ins = mm(G[:, 0:D], OT[p][:, r, j * 128:j * 128 + 128], pw_sb[:, r, :],
                                 start=(r == 0), stop=(r == PAIRS - 1))
                ins.then_inc(filled[kind], 1)

            def side(tl):
                for tile in tl:
                    fill(*tile)

            def batch(b):
                for s, tl in enumerate(tiles(b)):
                    scores(b, s)
                    behind(b, s, TURN, turn_p)
                    behind(b, s, WEIGH, values)
                    side(tl)

            for step, tl in enumerate(first_front):
                side(tl)
                for c in embeddings_behind.get(step, ()):
                    embed(c)
            pe_.wait_ge(h_ready, B)
            pe_.wait_ge(ld_hot, 16)
            pe_.wait_ge(hot_placed, 2 * TC)
            pe_.wait_ge(val_split, 2)
            batch(Batch(0))
            pe_.wait_ge(ld_hot, 32)
            pe_.wait_ge(ld_proj, 32)
            with pe_.Fori(0, (B - 2) // 2) as i:
                batch(Batch(1, i))
                batch(Batch(2, i))
            batch(Batch(B - 1))
            last = Batch(B - 1)
            for s in (H, H + 1):
                behind(last, s, TURN, turn_p)
                behind(last, s, WEIGH, values)

            def turn_block(b):
                pe_.wait_ge(fn_ready, b.at(1, 1))
                wait(pe_, fx_lo, b.at(1))
                turn_x(x_bank(b)).then_inc(fx_full, 1)

            def hidden(b):
                pe_.wait_ge(fx_lo, b.at(1, 1))
                wait(pe_, g_ready, b.at(6, -6))
                for m in range(HID // 128):
                    ins = project(f1_bank(b, m)[:, (m % 2) * S:(m % 2) * S + S], False,
                                  slice(0, S), w_in, slice(m * 128, m * 128 + 128))
                    if m % 2 == 1:
                        ins.then_inc(f1_full, 1)

            def outputs(b):
                pe_.wait_ge(g_ready, b.at(6, 6))
                wait(pe_, o_ready[1 - b.par], b.half(1, b.par))
                for t in range(TC):
                    for m in range(HID // 128):
                        ins = mm(bank[7][:, t * D:t * D + D], gT[b.par][:, m, t * 128:t * 128 + 128], w2_sb[:, m, :],
                                 start=(m == 0), stop=(m == HID // 128 - 1))
                ins.then_inc(f2_full, 1)

            def block_ff(b):
                if b.exists(2):
                    turn_block(b.after(2))
                outputs(b)
                if b.exists(2):
                    hidden(b.after(2))

            pe_.wait_ge(moved["r0"], TILES["r0"] * B)
            for tl in last_c0:
                side(tl)
            turn_block(Batch(0))
            behind(last, H + 2, WEIGH, values)
            pe_.wait_ge(ffn_split, 4)
            hidden(Batch(0))
            for tl in last_rel:
                side(tl)
            turn_block(Batch(1))
            for tl in last_out:
                side(tl)
            pe_.wait_ge(moved["o"], TC * B - 1)
            hidden(Batch(1))
            pe_.wait_ge(ld_w2, 16)
            pe_.wait_ge(moved["o"], TC * B)
            for p in range(2):
                block_ff(Batch(p))
            with pe_.Fori(0, B // 2 - 2) as i:
                for p in range(2):
                    block_ff(Batch(2 + p, i))
            for k in (B - 2, B - 1):
                block_ff(Batch(k))


def rel_windows(table, n):
    q, k = np.arange(n)[:, None], np.arange(n)[None, :]
    return table[np.clip(k - q, -MAX_REL, MAX_REL) + MAX_REL + 1]


def kernel(**inputs):
    import concourse.bacc as bacc
    from concourse.bass_utils import run_bass_kernel_spmd

    a = {k.split("_", 2)[-1] if k.startswith("L0_") else k: np.asarray(v) for k, v in inputs.items()}
    code = np.arange(VOCAB - a["special_W"].shape[0])
    etab = np.concatenate([
        np.concatenate([a["color_W"][code // 16], a["shape_W"][code % 16 // 4], a["quantity_W"][code % 4]], axis=-1),
        a["special_W"]])
    even = np.arange(0, D, 2, dtype=np.float32)
    angle = np.arange(S, dtype=np.float32)[:, None] * np.exp(-(even / np.float32(D)) * np.float32(math.log(10000.0)))
    pe = np.stack([np.sin(angle), np.cos(angle)], axis=-1).reshape(S, D).astype(np.float32)

    key_rel = np.zeros((NGRP + 2, REL, DH), np.float32)
    key_rel[:ROWS, :ROWS] = rel_windows(a["tab_kv"], ROWS)
    key_rel[ROWS:NGRP, :SIDE] = rel_windows(a["tab_kh"], SIDE)
    key_rel[NGRP, :ROWS] = a["tab_kv"][0]
    key_rel[NGRP + 1, :SIDE] = a["tab_kh"][0]
    val_rel = np.zeros((NGRP + 1, REL, DH), np.float32)
    val_rel[:ROWS, :ROWS] = rel_windows(a["tab_vv"], ROWS)
    val_rel[ROWS:NGRP, ROWS:] = rel_windows(a["tab_vh"], SIDE)
    val_rel[NGRP, :ROWS] = a["tab_vv"][0]
    val_rel[NGRP, ROWS:] = a["tab_vh"][0]
    token = np.arange(1, S)
    hot = np.zeros((S, REL), np.float32)
    hot[token, (token - 1) // SIDE] = 1.0
    hot[token, ROWS + (token - 1) % SIDE] = 1.0

    arrays = {
        "tok": a["x"],
        "etab": etab,
        "pe": pe,
        "qkw": a["qkv_w"].T,
        "proj_w": a["proj_w"].T,
        "proj_b": a["proj_b"],
        "key_rel": key_rel.transpose(2, 0, 1),
        "key_t0": np.stack([a["tab_kv"][0], a["tab_kh"][0]], axis=1),
        "val_rel": val_rel.transpose(1, 0, 2).reshape(REL, -1),
        "val_t0": np.stack([a["tab_vv"][0], a["tab_vh"][0]]),
        "key_hot": hot.T,
        "val_hot": hot,
        "ident": np.eye(128, dtype=np.float32),
        "w1": a["in_weight"].T,
        "b1": a["in_bias"].reshape(HID // 128, 128).T,
        "w2": a["out_weight"],
    }
    nc = bacc.Bacc("TRN2", target_bir_lowering=False, num_devices=1)
    arrays = {k: np.ascontiguousarray(v) for k, v in arrays.items()}
    args = [nc.dram_tensor("in_" + k, v.shape, mybir.dt.from_np(v.dtype), kind="ExternalInput").ap()
            for k, v in arrays.items()]
    args.append(nc.dram_tensor("out", (B, S, D), F32, kind="ExternalOutput").ap())
    build(nc, *args)
    r = run_bass_kernel_spmd(nc, [{"in_" + k: v for k, v in arrays.items()}], core_ids=[0])
    return r.results[0]["out"]
```
